# Optimizing a Trainium2 kernel written in Bass

```python
import numpy as np
import jax
import jax.numpy as jnp

def _softmax(x, axis=-1):
    return jax.nn.softmax(x, axis=axis)

def _gelu(x):
    return jax.nn.gelu(x, approximate=True)

def _silu(x):
    return jax.nn.silu(x)

def _sigmoid(x):
    return jax.nn.sigmoid(x)

def _layernorm(x, axis=-1, eps=1e-05):
    m = jnp.mean(x, axis=axis, keepdims=True)
    v = jnp.var(x, axis=axis, keepdims=True)
    return (x - m) / jnp.sqrt(v + eps)

def _scatter_add(tgt, idx, src, axis=0):
    return tgt.at[idx].add(src)

def _segment_sum(src, seg, n):
    return jax.ops.segment_sum(src, seg, n)
kernel_name = 'mk_xattn_ffn_d1_seqx_r8_f614dd'

def setup_inputs(seed: int=0):
    np.random.seed(seed)
    _w = jnp.asarray

    def _rec_inputs():
        import jax
        import jax.numpy as jnp
        _rk = jax.random.key(seed)
        x = -0.0003929 + 0.9999 * jax.random.normal(jax.random.fold_in(_rk, 1), (16, 64, 512), jnp.float32)
        _lenS = 64 - jax.random.randint(jax.random.fold_in(_rk, 7), (16,), 0, max(1, 64 // 4) + 1, jnp.int32)
        _lenS2 = 64 - jax.random.randint(jax.random.fold_in(_rk, 8), (16,), 0, max(1, 64 // 4) + 1, jnp.int32)
        _ctx_4096P = jax.random.normal(jax.random.fold_in(_rk, 11), (16, 16, 512), jnp.float32)
        _ctx_4096c = jax.random.dirichlet(jax.random.fold_in(_rk, 511), 0.3 * jnp.ones((16,), jnp.float32), (16, 64))
        _ctx_4096t = jnp.einsum('bsk,bkd->bsd', _ctx_4096c, _ctx_4096P)
        _ctx_4096t = _ctx_4096t * jax.lax.rsqrt(jnp.mean(jnp.square(_ctx_4096t)) + 1e-12) * 0.953939
        ctx_4096 = 2.81802e-05 + 1.00001 * (_ctx_4096t + 0.3 * jax.random.normal(jax.random.fold_in(_rk, 611), (16, 64, 512), jnp.float32))
        itok_BxS2_0_2047 = jax.random.randint(jax.random.fold_in(_rk, 12), (16, 64), 0, 256, jnp.int32)
        return (x, ctx_4096, itok_BxS2_0_2047)
    x, ctx_4096, itok_BxS2_0_2047 = _rec_inputs()

    def _L0_xattn_setup():
        import jax, jax.numpy as jnp
        import numpy as np
        HIDDEN = 512
        N_HEADS = 32
        N_KV_HEADS = 8
        HEAD_DIM = HIDDEN // N_HEADS
        N_REP = N_HEADS // N_KV_HEADS
        ROPE_THETA = 10000.0
        B, S = (2, 256)

        def _rotate_half(x):
            x1, x2 = jnp.split(x, 2, axis=-1)
            return jnp.concatenate((-x2, x1), axis=-1)

        def _rope_cos_sin(position_ids):
            inv_freq = 1.0 / ROPE_THETA ** (jnp.arange(0, HEAD_DIM, 2, dtype=jnp.float32) / HEAD_DIM)
            freqs = position_ids[..., None].astype(jnp.float32) * inv_freq
            emb = jnp.concatenate((freqs, freqs), axis=-1)
            return (jnp.cos(emb)[:, None, :, :], jnp.sin(emb)[:, None, :, :])
        key = jax.random.key(seed)
        ks = jax.random.split(key, 9)
        sc = 1.0 / np.sqrt(HIDDEN)
        query = jax.random.normal(ks[0], (B, S, HIDDEN), jnp.float32)
        key_t = jax.random.normal(ks[1], (B, S, HIDDEN), jnp.float32)
        value = jax.random.normal(ks[2], (B, S, HIDDEN), jnp.float32)
        position_ids = jnp.sort(jax.random.randint(ks[3], (B, S), 0, S), axis=-1)
        Wq = jax.random.normal(ks[4], (HIDDEN, N_HEADS * HEAD_DIM), jnp.float32) * sc
        Wk = jax.random.normal(ks[5], (HIDDEN, N_KV_HEADS * HEAD_DIM), jnp.float32) * sc
        Wv = jax.random.normal(ks[6], (HIDDEN, N_KV_HEADS * HEAD_DIM), jnp.float32) * sc
        Wo = jax.random.normal(ks[7], (N_HEADS * HEAD_DIM, HIDDEN), jnp.float32) * sc
        return {'query': query, 'key': key_t, 'value': value, 'position_ids': position_ids, 'Wq': Wq, 'Wk': Wk, 'Wv': Wv, 'Wo': Wo}
    _L0_xattn_all = _L0_xattn_setup()
    _L0_xattn_in = {k: v for k, v in _L0_xattn_all.items() if k in ('Wq', 'Wk', 'Wv', 'Wo')}
    del _L0_xattn_all

    def _L0_ffn_setup():
        import jax, jax.numpy as jnp
        import numpy as np
        IN_F = 512
        OUT_F = 512
        RANK = 8
        NUM_EXPERTS = 64
        TOP_K = 16
        ROUTER_DIM = 16
        ALPHA = 32
        SCALING = ALPHA / TOP_K
        BOTTLENECK = NUM_EXPERTS * RANK
        key = jax.random.key(seed)
        ks = jax.random.split(key, 5)
        x = jax.random.normal(ks[0], (4, 512, IN_F), dtype=jnp.float32)
        bound_a = float(np.sqrt(6.0 / IN_F))
        A_w = jax.random.uniform(ks[1], (BOTTLENECK, IN_F), jnp.float32, -bound_a, bound_a)
        B_w = jax.random.normal(ks[2], (OUT_F, BOTTLENECK), dtype=jnp.float32) * 0.02
        Wq_w = jax.random.normal(ks[3], (ROUTER_DIM, IN_F), dtype=jnp.float32) * 0.02
        keys = jax.random.normal(ks[4], (NUM_EXPERTS, ROUTER_DIM), dtype=jnp.float32) * 0.01
        return {'x': x, 'A_w': A_w, 'B_w': B_w, 'Wq_w': Wq_w, 'keys': keys}
    _L0_ffn_all = _L0_ffn_setup()
    _L0_ffn_in = {k: v for k, v in _L0_ffn_all.items() if k in ('A_w', 'B_w', 'Wq_w', 'keys')}
    del _L0_ffn_all
    return {'x': x, 'ctx_4096': ctx_4096, 'itok_BxS2_0_2047': itok_BxS2_0_2047, 'L0_xattn_Wq': _L0_xattn_in['Wq'], 'L0_xattn_Wk': _L0_xattn_in['Wk'], 'L0_xattn_Wv': _L0_xattn_in['Wv'], 'L0_xattn_Wo': _L0_xattn_in['Wo'], 'L0_ffn_A_w': _L0_ffn_in['A_w'], 'L0_ffn_B_w': _L0_ffn_in['B_w'], 'L0_ffn_Wq_w': _L0_ffn_in['Wq_w'], 'L0_ffn_keys': _L0_ffn_in['keys']}

def reference(x, ctx_4096, itok_BxS2_0_2047, L0_xattn_Wq, L0_xattn_Wk, L0_xattn_Wv, L0_xattn_Wo, L0_ffn_A_w, L0_ffn_B_w, L0_ffn_Wq_w, L0_ffn_keys):
    import jax
    import jax.numpy as jnp

    def _L0_xattn_ref(query, key, value, position_ids, Wq, Wk, Wv, Wo):
        import jax, jax.numpy as jnp
        import numpy as np
        HIDDEN = 512
        N_HEADS = 32
        N_KV_HEADS = 8
        HEAD_DIM = HIDDEN // N_HEADS
        N_REP = N_HEADS // N_KV_HEADS
        ROPE_THETA = 10000.0
        B, S = (2, 256)

        def _rotate_half(x):
            x1, x2 = jnp.split(x, 2, axis=-1)
            return jnp.concatenate((-x2, x1), axis=-1)

        def _rope_cos_sin(position_ids):
            inv_freq = 1.0 / ROPE_THETA ** (jnp.arange(0, HEAD_DIM, 2, dtype=jnp.float32) / HEAD_DIM)
            freqs = position_ids[..., None].astype(jnp.float32) * inv_freq
            emb = jnp.concatenate((freqs, freqs), axis=-1)
            return (jnp.cos(emb)[:, None, :, :], jnp.sin(emb)[:, None, :, :])
        nb, q_len, _ = query.shape
        q = jnp.einsum('bse,ef->bsf', query, Wq).reshape(nb, q_len, N_HEADS, HEAD_DIM).transpose(0, 2, 1, 3)
        k = jnp.einsum('bse,ef->bsf', key, Wk).reshape(nb, q_len, N_KV_HEADS, HEAD_DIM).transpose(0, 2, 1, 3)
        v = jnp.einsum('bse,ef->bsf', value, Wv).reshape(nb, q_len, N_KV_HEADS, HEAD_DIM).transpose(0, 2, 1, 3)
        cos, sin = _rope_cos_sin(position_ids)
        q = q * cos + _rotate_half(q) * sin
        k = k * cos + _rotate_half(k) * sin
        k = jnp.repeat(k, N_REP, axis=1)
        v = jnp.repeat(v, N_REP, axis=1)
        scale = 1.0 / jnp.sqrt(jnp.asarray(HEAD_DIM, q.dtype))
        scores = jnp.einsum('bhqd,bhkd->bhqk', q, k) * scale
        probs = jax.nn.softmax(scores, axis=-1)
        ctx = jnp.einsum('bhqk,bhkd->bhqd', probs, v)
        ctx = ctx.transpose(0, 2, 1, 3).reshape(nb, q_len, N_HEADS * HEAD_DIM)
        return jnp.einsum('bsf,fe->bse', ctx, Wo)

    def _L0_ffn_ref(x, A_w, B_w, Wq_w, keys):
        import jax, jax.numpy as jnp
        import numpy as np
        IN_F = 512
        OUT_F = 512
        RANK = 8
        NUM_EXPERTS = 64
        TOP_K = 16
        ROUTER_DIM = 16
        ALPHA = 32
        SCALING = ALPHA / TOP_K
        BOTTLENECK = NUM_EXPERTS * RANK
        q = jnp.einsum('bsd,rd->bsr', x, Wq_w)
        scores = jnp.einsum('bsr,er->bse', q, keys)
        top_vals, top_idx = jax.lax.top_k(scores, TOP_K)
        top_w = jax.nn.softmax(top_vals, axis=-1)
        gate = jnp.sum(jax.nn.one_hot(top_idx, NUM_EXPERTS, dtype=top_w.dtype) * top_w[..., None], axis=-2)
        z = jnp.einsum('bsd,nd->bsn', x, A_w)
        z = z.reshape(*z.shape[:-1], NUM_EXPERTS, RANK)
        z_gated = (z * gate[..., None]).reshape(*z.shape[:-2], BOTTLENECK)
        out = jnp.einsum('bsn,on->bso', z_gated, B_w) * SCALING
        return out
    x = x + _L0_xattn_ref(_layernorm(x, axis=-1), ctx_4096, ctx_4096, itok_BxS2_0_2047, L0_xattn_Wq, L0_xattn_Wk, L0_xattn_Wv, L0_xattn_Wo)
    x = x + _L0_ffn_ref(_layernorm(x, axis=-1), L0_ffn_A_w, L0_ffn_B_w, L0_ffn_Wq_w, L0_ffn_keys)
    return x

_drawn_inputs = setup_inputs


def setup_inputs(seed=0):
    import zlib

    import numpy as np

    out = dict(_drawn_inputs(seed))
    spreads = {}
    factors = {}
    for name, (base, spread) in spreads.items():
        noise = np.random.default_rng([zlib.crc32(name.encode()), seed]).standard_normal(out[name].shape)
        drawn = base * np.exp(spread * noise) if base else spread * noise
        out[name] = jnp.asarray(drawn.astype(out[name].dtype))
    for name, factor in factors.items():
        out[name] = (out[name] * factor).astype(out[name].dtype)
    return out
```

```python
import numpy as np
import concourse.bass as bass
from concourse import mybir
from contextlib import ExitStack

F32 = mybir.dt.float32
F32R = mybir.dt.float32r
I32 = mybir.dt.int32
ALU = mybir.AluOpType
ACT = mybir.ActivationFunctionType
AX = mybir.AxisListType

P = 128
BATCH = 64
D = 512
DK = D // P
HD = 16
KVH = 8
REP = 4
PAIRS = KVH // 2
KV = KVH * HD
E = 64
RANK = 8
TOP = 16
ROUTER = 16
AM = E + D
HALF = AM // 2
E0 = (HALF - E) // RANK
TOKENS = 1024
T = TOKENS // P
U = 4
EPS = 1e-5
SCALE = float(HD) ** -0.5
GATE_SCALE = 32 / TOP
STEPS = 11
TAKEN = -3.0e38
MAGIC = 1.5 * 2.0 ** 23
TWO_PI = 2 * np.pi
PI_A = float(np.round(TWO_PI * 2 ** 8) / 2 ** 8)
PI_B = float(np.round((TWO_PI - PI_A) * 2 ** 20) / 2 ** 20)
PI_C = float(np.float32(TWO_PI - PI_A - PI_B))
PI_LOW = float(np.nextafter(np.float32(np.pi), np.float32(0)))


def nth(per, t, k):
    return per * t + k


def build(nc, x, xT, cT, pos, wq, wkv, wo, aT, wr, keysT, bT, out):
    ctx = ExitStack()
    with ctx:
        def sb(name, shape, dt=F32):
            return ctx.enter_context(nc.sbuf_tensor(name, shape, dt))

        def pb(name, shape):
            return ctx.enter_context(nc.psum_tensor(name, shape, F32))

        def sem(name):
            return ctx.enter_context(nc.semaphore(name))

        x_sb = sb("x_sb", [P, T, D])
        xT_in = sb("xT_in", [P, DK, P])
        cT_in = sb("cT_in", [P, DK, P])
        wq_sb = sb("wq_sb", [P, DK, D])
        wkv_sb = sb("wkv_sb", [P, DK, 2 * KV])
        wo_sb = sb("wo_sb", [P, REP, D])
        am_sb = sb("am_sb", [P, DK, AM])
        wr_sb = sb("wr_sb", [ROUTER, D])
        keysT_sb = sb("keysT_sb", [ROUTER, E])
        pos_sb = sb("pos_sb", [P, T], I32)
        wq_hi, wq_lo = sb("wq_hi", [P, DK, D], F32R), sb("wq_lo", [P, DK, D], F32R)
        wkv_hi, wkv_lo = sb("wkv_hi", [P, DK, 2 * KV], F32R), sb("wkv_lo", [P, DK, 2 * KV], F32R)
        wo_hi, wo_lo = sb("wo_hi", [P, REP, D], F32R), sb("wo_lo", [P, REP, D], F32R)
        am_hi, am_lo = sb("am_hi", [P, DK, AM], F32R), sb("am_lo", [P, DK, AM], F32R)
        b_hi, b_lo = sb("b_hi", [P, DK, D], F32R), sb("b_lo", [P, DK, D], F32R)
        b_sb = wq_sb
        ident = sb("ident", [P, P])
        mean_w = sb("mean_w", [P, P])
        ones_bd = sb("ones_bd", [P, 2 * HD])
        head_mask = sb("head_mask", [P, KVH])
        freq = sb("freq", [P, HD // 2])
        half_pi = sb("half_pi", [P, 1])
        neg_half = sb("neg_half", [P, 1])
        pos_f = sb("pos_f", [P, T])
        ang = sb("ang", [P, T, HD // 2])
        turns = sb("turns", [P, T, HD // 2])
        rem = sb("rem", [P, 3, T, HD // 2])
        abs_r = sb("abs_r", [P, T, HD // 2])
        cs = sb("cs", [P, T, 2 * HD])
        cs_q = sb("cs_q", [P, 2 * HD])
        xT_hi, xT_lo = sb("xT_hi", [P, DK, P], F32R), sb("xT_lo", [P, DK, P], F32R)
        cT_hi, cT_lo = sb("cT_hi", [P, DK, P], F32R), sb("cT_lo", [P, DK, P], F32R)
        bn1, mv1, ve1, rstd1 = sb("bn1", [P, 6]), sb("mv1", [P, 2]), sb("ve1", [P, 1]), sb("rstd1", [P, 1])
        q_a, q_b, q_r = sb("q_a", [P, D]), sb("q_b", [P, D]), sb("q_r", [P, D])
        k_a, k_b, k_r = sb("k_a", [P, KV]), sb("k_b", [P, KV]), sb("k_r", [P, KV])
        v_st = sb("v_st", [P, KV])
        kT_hi, kT_lo = sb("kT_hi", [P, P], F32R), sb("kT_lo", [P, P], F32R)
        qT_hi, qT_lo = sb("qT_hi", [P, 2, REP, BATCH], F32R), sb("qT_lo", [P, 2, REP, BATCH], F32R)
        k_bd_hi = sb("k_bd_hi", [P, 2, KVH, BATCH], F32R)
        k_bd_lo = sb("k_bd_lo", [P, 2, KVH, BATCH], F32R)
        v_bd = sb("v_bd", [P, 2, PAIRS, 2 * HD])
        row_max = sb("row_max", [P, U, KVH])
        diff = sb("diff", [P, 2, D])
        pT = sb("pT", [P, 2, PAIRS, REP * BATCH])
        inv_sum = sb("inv_sum", [P, REP * BATCH])
        oT = sb("oT", [P, REP, 2, BATCH])
        oT_hi, oT_lo = sb("oT_hi", [P, REP, P], F32R), sb("oT_lo", [P, REP, P], F32R)
        bn2, mv2, ve2, rstd2 = sb("bn2", [P, 6]), sb("mv2", [P, 2]), sb("ve2", [P, 1]), sb("rstd2", [P, 1])
        x2 = sb("x2", [P, D])
        x2T_hi, x2T_lo = sb("x2T_hi", [P, DK, P], F32R), sb("x2T_lo", [P, DK, P], F32R)
        s_sb, s_a, s_b = sb("s_sb", [P, E]), sb("s_a", [P, E]), sb("s_b", [P, E])
        top_a, top_b = sb("top_a", [P, 8]), sb("top_b", [P, 8])
        neg_max, e_sum, e_inv, g_scale = (sb(n, [P, 1]) for n in ("neg_max", "e_sum", "e_inv", "g_scale"))
        e_sb, e_top, gate = sb("e_sb", [P, E]), sb("e_top", [P, E]), sb("gate", [P, E])
        zg = sb("zg", [P, D])
        zT_hi, zT_lo = sb("zT_hi", [P, DK, P], F32R), sb("zT_lo", [P, DK, P], F32R)
        res = sb("res", [P, D])

        ps_s = pb("ps_s", [P, 2, D])
        ps_d = pb("ps_d", [P, D])
        ps_o = pb("ps_o", [P, D])
        ps_w0, ps_w1 = pb("ps_w0", [P, D]), pb("ps_w1", [P, D])
        ps_t0, ps_t1 = pb("ps_t0", [P, D]), pb("ps_t1", [P, D])
        MEAN_A, MEAN_B = ps_s[:, 1, 0:HALF], ps_d[:, 0:HALF]

        ld = {n: sem("ld_" + n) for n in ("c", "x", "xnat0", "xnat", "pos", "wq", "wkv", "wo", "am",
                                           "wr", "keys", "b")}
        const_ok = sem("const_ok")
        mask_step = sem("mask_step")
        rope_step = sem("rope_step")
        abs_ok = sem("abs_ok")
        cs_ok = sem("cs_ok")
        mean_q = sem("mean_q")
        wq_cent = sem("wq_cent")
        wq_h, wq_l = sem("wq_h"), sem("wq_l")
        wkv_h, wkv_l = sem("wkv_h"), sem("wkv_l")
        wo_h, wo_l = sem("wo_h"), sem("wo_l")
        route_w = sem("route_w")
        mean_am = sem("mean_am")
        am_cent = sem("am_cent")
        am_h, am_l = sem("am_h"), sem("am_l")
        b_h, b_l = sem("b_h"), sem("b_l")
        c_hi_ok, c_lo_ok, x_hi_ok, x_lo_ok = sem("c_hi_ok"), sem("c_lo_ok"), sem("x_hi_ok"), sem("x_lo_ok")
        stat1 = sem("stat1")
        rstd1_ok = sem("rstd1_ok")
        cs_q_ok = sem("cs_q_ok")
        kv_ps, q_ps = sem("kv_ps"), sem("q_ps")
        k_rot = sem("k_rot")
        v_st_ok = sem("v_st_ok")
        q_rot = sem("q_rot")
        q_r_ok = sem("q_r_ok")
        kT_ps, qT_ps = sem("kT_ps"), sem("qT_ps")
        kT_hi_ok, kT_lo_ok = sem("kT_hi_ok"), sem("kT_lo_ok")
        qT_hi_ok, qT_lo_ok = sem("qT_hi_ok"), sem("qT_lo_ok")
        k_bd_ok = sem("k_bd_ok")
        v_bd_ok = sem("v_bd_ok")
        s_ps = sem("s_ps")
        max_ok = sem("max_ok")
        diff_ok = sem("diff_ok")
        dT_ps = sem("dT_ps")
        exp_ok = sem("exp_ok")
        o_ps = sem("o_ps")
        inv_ok = sem("inv_ok")
        oT_ok = sem("oT_ok")
        oT_hi_ok, oT_lo_ok = sem("oT_hi_ok"), sem("oT_lo_ok")
        y_ps = sem("y_ps")
        x2_ok = sem("x2_ok")
        stat2 = sem("stat2")
        rstd2_ok = sem("rstd2_ok")
        x2T_ps, x2T_hi_ok, x2T_lo_ok = sem("x2T_ps"), sem("x2T_hi_ok"), sem("x2T_lo_ok")
        z_ps = sem("z_ps")
        s_ok = sem("s_ok")
        top_step = sem("top_step")
        e_ok = sem("e_ok")
        zg_ok = sem("zg_ok")
        zT_ps, zT_hi_ok, zT_lo_ok = sem("zT_ps"), sem("zT_hi_ok"), sem("zT_lo_ok")
        out_ps = sem("out_ps")
        res_ok = sem("res_ok")
        stored = sem("stored")

        block = ctx.enter_context(nc.Block())

        def pipeline(eng, step, between=None):
            def tiles(i):
                return [t if 0 <= t < T else None for t in (i + 1, i, i - 1, i - 2)]
            between = between or {}
            for i in (-1, 0, 1):
                if i in between:
                    between[i]()
                step(*tiles(i))
            if 2 in between:
                between[2]()
            with eng.Fori(2, T - 1) as i:
                step(i + 1, i, i - 1, i - 2)
            for i in range(T - 1, T + 2):
                step(*tiles(i))

        @block.sync
        def _(sp):
            def load(dst, src, name):
                sp.dma_start(dst, src).then_inc(ld[name], 16)

            load(wkv_sb[:], wkv, "wkv")
            load(cT_in[:], cT[0], "c")
            load(wq_sb[:], wq, "wq")
            load(xT_in[:], xT[0], "x")
            load(pos_sb[:], pos, "pos")
            load(x_sb[:, 0, :], x[0], "xnat0")
            load(wr_sb[:], wr, "wr")
            load(keysT_sb[:], keysT, "keys")
            load(wo_sb[:], wo, "wo")
            load(am_sb[:, :, E:AM], aT, "am")
            load(x_sb[:, 1:T, :], x[1:T].rearrange("t p d -> p t d"), "xnat")

            def load_tile(t):
                sp.wait_ge(c_hi_ok, t)
                sp.wait_ge(c_lo_ok, t)
                load(cT_in[:], cT[t], "c")
                sp.wait_ge(x_hi_ok, t)
                sp.wait_ge(x_lo_ok, t)
                load(xT_in[:], xT[t], "x")

            def store_tile(t):
                sp.wait_ge(res_ok, t + 1)
                sp.dma_start(out[t], res[:]).then_inc(stored, 16)

            with sp.Fori(1, 4) as t:
                load_tile(t)
            with sp.Fori(4, T) as t:
                load_tile(t)
                store_tile(t - 4)
            with sp.Fori(T - 4, T) as t:
                store_tile(t)
            sp.wait_ge(stored, 16 * T)

        @block.gpsimd
        def _(pool):
            pool.memset(half_pi[:], float(np.pi / 2)).then_inc(const_ok, 1)
            pool.memset(neg_half[:], -0.5).then_inc(const_ok, 1)
            for j in range(HD // 2):
                f = np.float32(1.0) / np.float32(10000.0) ** np.float32(2 * j / HD)
                pool.memset(freq[:, j:j + 1], float(f)).then_inc(const_ok, 1)
            pool.memset(mean_w[:], 1.0 / D).then_inc(const_ok, 1)
            pool.memset(ones_bd[:], 0.0).then_inc(mask_step, 1)
            pool.memset(v_bd[:], 0.0).then_inc(mask_step, 1)
            pool.memset(head_mask[:], 1.0).then_inc(mask_step, 1)
            pool.memset(ident[:], 0.0).then_inc(mask_step, 1)
            pool.wait_ge(mask_step, 4)
            for h in range(2):
                pool.memset(ones_bd[BATCH * h:BATCH * (h + 1), HD * h:HD * (h + 1)], 1.0).then_inc(const_ok, 1)
                pool.wait_ge(const_ok, 12 + h)
            pool.affine_select(out=ident[:], in_=ident[:], compare_op=ALU.not_equal, fill=1.0, base=0,
                               pattern=[[-1, P]], channel_multiplier=1).then_inc(const_ok, 1)
            pool.affine_select(out=head_mask[:], in_=head_mask[:], compare_op=ALU.is_ge, fill=0.0, base=0,
                               pattern=[[-HD, KVH]], channel_multiplier=1).then_inc(mask_step, 1)
            pool.wait_ge(mask_step, 5)
            pool.affine_select(out=head_mask[:], in_=head_mask[:], compare_op=ALU.is_ge, fill=0.0, base=HD - 1,
                               pattern=[[HD, KVH]], channel_multiplier=-1).then_inc(const_ok, 1)
            for k in range(DK):
                pool.wait_ge(wkv_h, k + 1)
                pool.tensor_tensor(wkv_lo[:, k, :], wkv_sb[:, k, :], wkv_hi[:, k, :].bitcast(F32),
                                   ALU.subtract).then_inc(wkv_l, 1)

            def split_lo(lo, raw, hi, high, low, k):
                pool.wait_ge(high, k + 1)
                pool.tensor_tensor(lo[:, k, :], raw[:, k, :], hi[:, k, :].bitcast(F32),
                                   ALU.subtract).then_inc(low, 1)

            def step(p, a, f, g):
                if p is not None:
                    pool.wait_ge(c_hi_ok, nth(1, p, 1))
                    if not isinstance(p, int) or p >= 1:
                        pool.wait_ge(kv_ps, nth(1, p, 0))
                    pool.tensor_tensor(cT_lo[:], cT_in[:], cT_hi[:].bitcast(F32), ALU.subtract).then_inc(c_lo_ok, 1)
                    pool.wait_ge(x_hi_ok, nth(1, p, 1))
                    if not isinstance(p, int) or p >= 1:
                        pool.wait_ge(q_ps, nth(1, p, 0))
                    pool.tensor_tensor(xT_lo[:], xT_in[:], xT_hi[:].bitcast(F32), ALU.subtract).then_inc(x_lo_ok, 1)
                    pool.wait_ge(stat1, nth(3, p, 3))
                    if not isinstance(p, int) or p >= 1:
                        pool.wait_ge(cs_q_ok, nth(1, p, 0))
                    pool.tensor_tensor(rstd1[:], ve1[:], neg_half[:], ALU.pow).then_inc(rstd1_ok, 1)
                if f is not None:
                    pool.wait_ge(oT_hi_ok, nth(1, f, 1))
                    if not isinstance(f, int) or f >= 1:
                        pool.wait_ge(y_ps, nth(1, f, 0))
                    pool.tensor_tensor(oT_lo[:], oT[:].rearrange("p r b q -> p r (b q)"), oT_hi[:].bitcast(F32),
                                       ALU.subtract).then_inc(oT_lo_ok, 1)
                if p is not None:
                    pool.wait_ge(q_rot, nth(2, p, 2))
                    if not isinstance(p, int) or p >= 1:
                        pool.wait_ge(qT_ps, nth(1, p, 0))
                    pool.tensor_tensor(q_r[:].rearrange("p (r k d) -> p k r d", r=REP, k=KVH),
                                       q_a[:].rearrange("p (k r d) -> p k r d", r=REP, k=KVH),
                                       q_b[:].rearrange("p (k r d) -> p k r d", r=REP, k=KVH),
                                       ALU.add).then_inc(q_r_ok, 1)
                    for n, (bd, kT, ok) in enumerate(((k_bd_hi, kT_hi, kT_hi_ok), (k_bd_lo, kT_lo, kT_lo_ok))):
                        pool.wait_ge(ok, nth(1, p, 1))
                        if n == 0 and a is not None:
                            pool.wait_ge(s_ps, nth(U, a, U))
                        pool.tensor_tensor(
                            bd[:],
                            kT[:].bitcast(F32).rearrange("p (b q) -> p b q", b=2).unsqueeze(2)
                            .broadcast_to([P, 2, KVH, BATCH]),
                            head_mask[:].unsqueeze(1).unsqueeze(3).broadcast_to([P, 2, KVH, BATCH]),
                            ALU.mult).then_inc(k_bd_ok, 1)
                if f is not None:
                    pool.wait_ge(stat2, nth(3, f, 3))
                    if not isinstance(f, int) or f >= 1:
                        pool.wait_ge(top_step, nth(STEPS, f, 0))
                        pool.wait_ge(e_ok, nth(1, f, 0))
                    pool.tensor_tensor(rstd2[:], ve2[:], neg_half[:], ALU.pow).then_inc(rstd2_ok, 1)

            def wo_parts():
                for k in range(REP):
                    split_lo(wo_lo, wo_sb, wo_hi, wo_h, wo_l, k)

            def b_parts():
                for k in range(DK):
                    split_lo(b_lo, b_sb, b_hi, b_h, b_l, k)

            pipeline(pool, step, {0: wo_parts, 1: b_parts})

        @block.scalar
        def _(act):
            def load_b():
                act.wait_ge(wq_h, DK)
                act.wait_ge(wq_l, DK)
                act.dma_start(b_sb[:], bT).then_inc(ld["b"], 16)

            act.wait_ge(const_ok, 1)
            act.wait_ge(rope_step, 8)
            act.activation(abs_r[:], rem[:, 2], ACT.Abs).then_inc(abs_ok, 1)
            act.activation(cs[:, :, 24:32], rem[:, 2], ACT.Sin).then_inc(cs_ok, 1)
            act.activation(cs[:, :, 16:24], rem[:, 2], ACT.Sin, scale=-1.0).then_inc(cs_ok, 1)
            act.wait_ge(abs_ok, 1)
            for c in range(2):
                act.activation(cs[:, :, 8 * c:8 * c + 8], abs_r[:], ACT.Sin, scale=-1.0,
                               bias=half_pi[:]).then_inc(cs_ok, 1)
            act.wait_ge(ld["wkv"], 16)
            for k in range(DK):
                act.activation(wkv_hi[:, k, :], wkv_sb[:, k, :], ACT.Copy).then_inc(wkv_h, 1)
            for k in range(DK):
                act.wait_ge(wq_cent, k + 1)
                act.activation(wq_hi[:, k, :], wq_sb[:, k, :], ACT.Copy).then_inc(wq_h, 1)

            def step(p, a, f, g):
                if p is not None:
                    act.wait_ge(ld["c"], nth(16, p, 16))
                    if not isinstance(p, int) or p >= 1:
                        act.wait_ge(kv_ps, nth(1, p, 0))
                        act.wait_ge(c_lo_ok, nth(1, p, 0))
                    act.activation(cT_hi[:], cT_in[:], ACT.Copy).then_inc(c_hi_ok, 1)
                    act.wait_ge(ld["x"], nth(16, p, 16))
                    if not isinstance(p, int) or p >= 1:
                        act.wait_ge(q_ps, nth(1, p, 0))
                        act.wait_ge(x_lo_ok, nth(1, p, 0))
                    act.activation(xT_hi[:], xT_in[:], ACT.Copy).then_inc(x_hi_ok, 1)
                if a is not None:
                    act.wait_ge(v_st_ok, nth(1, a, 1))
                    if not isinstance(a, int) or a >= 1:
                        act.wait_ge(o_ps, nth(2, a, 0))
                    else:
                        act.wait_ge(mask_step, 4)
                    for b in range(2):
                        for h in range(2):
                            act.activation(
                                v_bd[BATCH * h:BATCH * (h + 1), b, :, HD * h:HD * (h + 1)],
                                v_st[BATCH * b:BATCH * (b + 1), :]
                                .rearrange("p (g h d) -> p g h d", g=PAIRS, h=2)[:, :, h, :],
                                ACT.Copy).then_inc(v_bd_ok, 1)

                def exp(u):
                    act.wait_ge(dT_ps, nth(U, a, u + 1))
                    b, rp = u // 2, u % 2
                    if not isinstance(a, int) or a >= 1:
                        act.wait_ge(o_ps, nth(2, a, b - 1))
                    act.activation(pT[:, b, :, P * rp:P * (rp + 1)],
                                   ps_d[:].rearrange("p (g q) -> p g q", g=PAIRS),
                                   ACT.Exp, scale=SCALE).then_inc(exp_ok, 1)

                if a is not None:
                    exp(0)
                if g is not None:
                    act.wait_ge(zT_ps, nth(1, g, 1))
                    act.activation(zT_hi[:], ps_t1[:].rearrange("p (k q) -> p k q", k=DK), ACT.Copy)\
                       .then_inc(zT_hi_ok, 1)
                if a is not None:
                    exp(1)
                if p is not None:
                    act.wait_ge(k_rot, nth(3, p, 2))
                    act.wait_ge(kv_ps, nth(1, p, 1))
                    if a is not None:
                        act.wait_ge(v_bd_ok, nth(4, a, 4))
                    act.activation(v_st[:], ps_w1[:, KV:2 * KV], ACT.Copy).then_inc(v_st_ok, 1)
                if f is not None:
                    act.wait_ge(oT_ok, nth(2, f, 2))
                    if not isinstance(f, int) or f >= 1:
                        act.wait_ge(y_ps, nth(1, f, 0))
                    act.activation(oT_hi[:], oT[:].rearrange("p r b q -> p r (b q)"), ACT.Copy)\
                       .then_inc(oT_hi_ok, 1)
                if a is not None:
                    exp(2)
                if p is not None:
                    act.wait_ge(kT_ps, nth(1, p, 1))
                    if not isinstance(p, int) or p >= 1:
                        act.wait_ge(k_bd_ok, nth(2, p, 0))
                    act.activation(kT_hi[:], ps_t1[:, 0:P], ACT.Copy).then_inc(kT_hi_ok, 1)
                if f is not None:
                    act.wait_ge(x2T_ps, nth(1, f, 1))
                    if not isinstance(f, int) or f >= 1:
                        act.wait_ge(z_ps, nth(2, f, 0))
                    act.activation(x2T_hi[:], ps_t0[:].rearrange("p (k q) -> p k q", k=DK), ACT.Copy)\
                       .then_inc(x2T_hi_ok, 1)
                if a is not None:
                    exp(3)
                if p is not None:
                    act.wait_ge(qT_ps, nth(1, p, 1))
                    if a is not None:
                        act.wait_ge(s_ps, nth(U, a, U))
                    act.activation(qT_hi[:].rearrange("p b r q -> p r b q"),
                                   ps_t0[:].rearrange("p (r b q) -> p r b q", r=REP, b=2),
                                   ACT.Copy).then_inc(qT_hi_ok, 1)
                if f is not None:
                    act.wait_ge(z_ps, nth(2, f, 1))
                    if not isinstance(f, int) or f >= 1:
                        act.wait_ge(top_step, nth(STEPS, f, 0))
                    act.activation(s_sb[:], ps_w0[:, 0:E], ACT.Copy).then_inc(s_ok, 1)
                    act.wait_ge(s_ok, nth(1, f, 1))
                    act.wait_ge(rstd2_ok, nth(1, f, 1))
                    act.wait_ge(top_step, nth(STEPS, f, 2))
                    act.activation(e_sb[:], s_sb[:], ACT.Exp, scale=rstd2[:], bias=neg_max[:]).then_inc(e_ok, 1)

            def later_weights():
                load_b()
                act.wait_ge(ld["wo"], 16)
                for k in range(REP):
                    act.activation(wo_hi[:, k, :], wo_sb[:, k, :], ACT.Copy).then_inc(wo_h, 1)
                act.wait_ge(route_w, 1)
                act.activation(am_sb[:, :, 0:E], ps_o[:, 0:DK * E].rearrange("p (k e) -> p k e", k=DK),
                               ACT.Copy).then_inc(route_w, 1)

            def down_weights():
                for k in range(DK):
                    act.wait_ge(am_cent, 2 * k + 2)
                    act.activation(am_hi[:, k, :], am_sb[:, k, :], ACT.Copy).then_inc(am_h, 1)
                act.wait_ge(ld["b"], 16)
                for k in range(DK):
                    act.activation(b_hi[:, k, :], b_sb[:, k, :], ACT.Copy).then_inc(b_h, 1)

            pipeline(act, step, {0: later_weights, 1: down_weights})

        @block.vector
        def _(dve):
            dve.wait_ge(ld["pos"], 16)
            dve.tensor_copy(pos_f[:], pos_sb[:]).then_inc(rope_step, 1)
            dve.wait_ge(rope_step, 1)
            dve.wait_ge(const_ok, 10)
            J = HD // 2
            dve.tensor_tensor(ang[:], pos_f[:].unsqueeze(2).broadcast_to([P, T, J]),
                              freq[:].unsqueeze(1).broadcast_to([P, T, J]), ALU.mult).then_inc(rope_step, 1)
            dve.wait_ge(rope_step, 2)
            dve.tensor_scalar(turns[:], ang[:], float(1 / TWO_PI), MAGIC, ALU.mult, ALU.add).then_inc(rope_step, 1)
            dve.wait_ge(rope_step, 3)
            dve.tensor_scalar(turns[:], turns[:], MAGIC, None, ALU.subtract).then_inc(rope_step, 1)
            dve.wait_ge(rope_step, 4)
            for n, (part, src) in enumerate(((PI_A, ang[:]), (PI_B, rem[:, 0]), (PI_C, rem[:, 1]))):
                dve.scalar_tensor_tensor(rem[:, n], turns[:], -part, src, ALU.mult, ALU.add)\
                   .then_inc(rope_step, 1)
                dve.wait_ge(rope_step, 5 + n)
            dve.tensor_scalar(rem[:, 2], rem[:, 2], PI_LOW, -PI_LOW, ALU.min, ALU.max).then_inc(rope_step, 1)

            dve.wait_ge(mean_q, 1)
            for k in range(DK):
                dve.tensor_tensor(wq_sb[:, k, :], wq_sb[:, k, :], ps_w0[:], ALU.subtract).then_inc(wq_cent, 1)

            def wq_low(k):
                dve.wait_ge(wq_h, k + 1)
                dve.tensor_tensor(wq_lo[:, k, :], wq_sb[:, k, :], wq_hi[:, k, :].bitcast(F32),
                                  ALU.subtract).then_inc(wq_l, 1)

            for k in range(DK):
                wq_low(k)

            def step(p, a, f, g):
                def unit(u, stats=False):
                    s = ps_s[:, u % 2, :].rearrange("p (h k) -> p h k", h=KVH)
                    dve.wait_ge(s_ps, nth(U, a, u + 1))
                    if stats:
                        dve.wait_ge(stat1, nth(3, p, 1))
                    dve.tensor_reduce(row_max[:, u, :], s, AX.X, ALU.max).then_inc(max_ok, 1)
                    dve.wait_ge(max_ok, nth(U, a, u + 1))
                    if not isinstance(a, int) or a >= 1 or u >= 2:
                        dve.wait_ge(dT_ps, nth(U, a, u - 1))
                    dve.tensor_tensor(diff[:, u % 2, :].rearrange("p (h k) -> p h k", h=KVH), s,
                                      row_max[:, u, :].unsqueeze(2).broadcast_to([P, KVH, BATCH]),
                                      ALU.subtract).then_inc(diff_ok, 1)

                def normalise(t, b):
                    dve.wait_ge(o_ps, nth(2, t, b + 1))
                    n = REP * BATCH
                    dve.reciprocal(inv_sum[:], ps_o[:, n:2 * n]).then_inc(inv_ok, 1)
                    dve.wait_ge(inv_ok, nth(2, t, b + 1))
                    if b == 0 and (not isinstance(t, int) or t >= 1):
                        dve.wait_ge(oT_lo_ok, nth(1, t, 0))
                    dve.tensor_tensor(oT[:, :, b, :], ps_o[:, 0:n].rearrange("p (r q) -> p r q", r=REP),
                                      inv_sum[:].rearrange("p (r q) -> p r q", r=REP),
                                      ALU.mult).then_inc(oT_ok, 1)

                if a is not None:
                    unit(0)
                if f is not None:
                    normalise(f, 1)
                if p is not None:
                    if isinstance(p, int) and p == 0:
                        dve.wait_ge(ld["xnat0"], 16)
                    else:
                        dve.wait_ge(ld["xnat"], 16)
                    dve.bn_stats(bn1[:], x_sb[:, p, :]).then_inc(stat1, 1)
                if a is not None:
                    unit(1, stats=p is not None)
                if p is not None:
                    if a is None:
                        dve.wait_ge(stat1, nth(3, p, 1))
                    dve.bn_aggr(mv1[:], bn1[:]).then_inc(stat1, 1)
                    dve.wait_ge(stat1, nth(3, p, 2))
                    if not isinstance(p, int) or p >= 1:
                        dve.wait_ge(rstd1_ok, nth(1, p, 0))
                    dve.tensor_scalar_add(ve1[:], mv1[:, 1:2], EPS).then_inc(stat1, 1)
                if g is not None:
                    dve.wait_ge(zT_hi_ok, nth(1, g, 1))
                    dve.tensor_tensor(zT_lo[:], ps_t1[:].rearrange("p (k q) -> p k q", k=DK),
                                      zT_hi[:].bitcast(F32), ALU.subtract).then_inc(zT_lo_ok, 1)
                if p is not None:
                    if isinstance(p, int) and p == 0:
                        dve.wait_ge(cs_ok, 4)
                    dve.wait_ge(kv_ps, nth(1, p, 1))
                    k_ps = ps_w1[:, 0:KV].rearrange("p (h s j) -> p h s j", h=KVH, s=2)
                    shape = [P, KVH, 2, J]

                    def table(t, at, n, h):
                        return t[:, at:at + HD].rearrange("p (s j) -> p s j", s=2).unsqueeze(1)\
                            .broadcast_to([P, h, 2, J])

                    dve.tensor_tensor(k_a[:].rearrange("p (h s j) -> p h s j", h=KVH, s=2), k_ps,
                                      table(cs[:, p, :], 0, HD, KVH), ALU.mult).then_inc(k_rot, 1)
                    dve.tensor_tensor(k_b[:].rearrange("p (h s j) -> p h s j", h=KVH, s=2), k_ps[:, :, ::-1, :],
                                      table(cs[:, p, :], HD, HD, KVH), ALU.mult).then_inc(k_rot, 1)
                    dve.wait_ge(k_rot, nth(3, p, 2))
                    if not isinstance(p, int) or p >= 1:
                        dve.wait_ge(kT_ps, nth(1, p, 0))
                    dve.tensor_tensor(k_r[:], k_a[:], k_b[:], ALU.add).then_inc(k_rot, 1)
                    dve.wait_ge(rstd1_ok, nth(1, p, 1))
                    if not isinstance(p, int) or p >= 1:
                        dve.wait_ge(q_rot, nth(2, p, 0))
                    dve.tensor_scalar_mul(cs_q[:], cs[:, p, :], rstd1[:]).then_inc(cs_q_ok, 1)
                if g is not None:
                    dve.wait_ge(out_ps, nth(1, g, 1))
                    if not isinstance(g, int) or g >= 1:
                        dve.wait_ge(stored, nth(16, g, 0))
                    dve.tensor_tensor(res[:], ps_w0[:], x2[:], ALU.add).then_inc(res_ok, 1)
                if a is not None:
                    unit(2)
                if p is not None:
                    dve.wait_ge(q_ps, nth(1, p, 1))
                    dve.wait_ge(cs_q_ok, nth(1, p, 1))
                    if not isinstance(p, int) or p >= 1:
                        dve.wait_ge(q_r_ok, nth(1, p, 0))
                    H = REP * KVH
                    w = ps_w0[:].rearrange("p (h s j) -> p h s j", h=H, s=2)
                    dve.tensor_tensor(q_a[:].rearrange("p (h s j) -> p h s j", h=H, s=2), w,
                                      table(cs_q, 0, HD, H), ALU.mult).then_inc(q_rot, 1)
                    dve.tensor_tensor(q_b[:].rearrange("p (h s j) -> p h s j", h=H, s=2), w[:, :, ::-1, :],
                                      table(cs_q, HD, HD, H), ALU.mult).then_inc(q_rot, 1)
                if a is not None:
                    unit(3)
                if f is not None:
                    dve.wait_ge(y_ps, nth(1, f, 1))
                    if not isinstance(f, int) or f >= 1:
                        dve.wait_ge(x2T_ps, nth(1, f, 0))
                        dve.wait_ge(res_ok, nth(1, f, 0))
                    dve.tensor_tensor(x2[:], ps_w1[:], x_sb[:, f, :], ALU.add).then_inc(x2_ok, 1)
                    dve.wait_ge(x2_ok, nth(1, f, 1))
                    dve.bn_stats(bn2[:], x2[:]).then_inc(stat2, 1)
                if f is not None and p is None:
                    dve.wait_ge(stat2, nth(3, f, 1))
                if p is not None:
                    if f is not None:
                        dve.wait_ge(stat2, nth(3, f, 1))
                    dve.wait_ge(kT_hi_ok, nth(1, p, 1))
                    if not isinstance(p, int) or p >= 1:
                        dve.wait_ge(k_bd_ok, nth(2, p, 0))
                    dve.tensor_tensor(kT_lo[:], ps_t1[:, 0:P], kT_hi[:].bitcast(F32), ALU.subtract)\
                       .then_inc(kT_lo_ok, 1)
                if f is not None:
                    dve.bn_aggr(mv2[:], bn2[:]).then_inc(stat2, 1)
                    dve.wait_ge(stat2, nth(3, f, 2))
                    if not isinstance(f, int) or f >= 1:
                        dve.wait_ge(rstd2_ok, nth(1, f, 0))
                    dve.tensor_scalar_add(ve2[:], mv2[:, 1:2], EPS).then_inc(stat2, 1)
                if a is not None:
                    normalise(a, 0)
                if f is not None:
                    dve.wait_ge(x2T_hi_ok, nth(1, f, 1))
                    dve.tensor_tensor(x2T_lo[:], ps_t0[:].rearrange("p (k q) -> p k q", k=DK),
                                      x2T_hi[:].bitcast(F32), ALU.subtract).then_inc(x2T_lo_ok, 1)
                if f is not None:
                    dve.wait_ge(s_ok, nth(1, f, 1))
                if p is not None:
                    dve.wait_ge(qT_hi_ok, nth(1, p, 1))
                    dve.tensor_tensor(qT_lo[:].rearrange("p b r q -> p r b q"),
                                      ps_t0[:].rearrange("p (r b q) -> p r b q", r=REP, b=2),
                                      qT_hi[:].bitcast(F32).rearrange("p b r q -> p r b q"),
                                      ALU.subtract).then_inc(qT_lo_ok, 1)
                if f is not None:
                    dve.max(top_a[:], s_sb[:]).then_inc(top_step, 1)
                    dve.wait_ge(rstd2_ok, nth(1, f, 1))
                    dve.wait_ge(top_step, nth(STEPS, f, 1))
                    dve.tensor_scalar(neg_max[:], top_a[:, 0:1], rstd2[:], -1.0, ALU.mult, ALU.mult)\
                       .then_inc(top_step, 1)
                    dve.match_replace(s_a[:], top_a[:], s_sb[:], TAKEN).then_inc(top_step, 1)
                    dve.wait_ge(top_step, nth(STEPS, f, 3))
                    dve.memset(e_top[:, 0:1], 0.0).then_inc(top_step, 1)
                    dve.max(top_b[:], s_a[:]).then_inc(top_step, 1)
                    dve.wait_ge(top_step, nth(STEPS, f, 5))
                    dve.memset(e_top[:, 1:2], 0.0).then_inc(top_step, 1)
                    dve.match_replace(s_b[:], top_b[:], s_a[:], TAKEN).then_inc(top_step, 1)
                    dve.wait_ge(top_step, nth(STEPS, f, 7))
                    dve.wait_ge(e_ok, nth(1, f, 1))
                    dve.scalar_tensor_tensor(e_top[:], s_b[:], TAKEN, e_sb[:], ALU.is_equal, ALU.mult,
                                             accum_out=e_sum[:]).then_inc(top_step, 1)
                    dve.wait_ge(top_step, nth(STEPS, f, 8))
                    dve.reciprocal(e_inv[:], e_sum[:]).then_inc(top_step, 1)
                    dve.wait_ge(top_step, nth(STEPS, f, 9))
                    dve.tensor_scalar(g_scale[:], e_inv[:], rstd2[:], GATE_SCALE, ALU.mult, ALU.mult)\
                       .then_inc(top_step, 1)
                    dve.wait_ge(top_step, nth(STEPS, f, 10))
                    dve.tensor_scalar_mul(gate[:], e_top[:], g_scale[:]).then_inc(top_step, 1)
                    dve.wait_ge(top_step, nth(STEPS, f, 11))
                    if not isinstance(f, int) or f >= 1:
                        dve.wait_ge(zT_ps, nth(1, f, 0))
                    n0 = E0 * RANK
                    dve.tensor_tensor(zg[:, 0:n0].rearrange("p (e r) -> p e r", r=RANK),
                                      ps_w0[:, E:HALF].rearrange("p (e r) -> p e r", r=RANK),
                                      gate[:, 0:E0].unsqueeze(2).broadcast_to([P, E0, RANK]),
                                      ALU.mult).then_inc(zg_ok, 1)
                    dve.wait_ge(z_ps, nth(2, f, 2))
                    dve.tensor_tensor(zg[:, n0:D].rearrange("p (e r) -> p e r", r=RANK),
                                      ps_w1[:, 0:HALF].rearrange("p (e r) -> p e r", r=RANK),
                                      gate[:, E0:E].unsqueeze(2).broadcast_to([P, E - E0, RANK]),
                                      ALU.mult).then_inc(zg_ok, 1)

            def am_centre():
                dve.wait_ge(mean_am, 1)
                for k in range(DK):
                    dve.tensor_tensor(am_sb[:, k, 0:HALF], am_sb[:, k, 0:HALF], MEAN_A, ALU.subtract)\
                       .then_inc(am_cent, 1)
                    dve.tensor_tensor(am_sb[:, k, HALF:AM], am_sb[:, k, HALF:AM], MEAN_B, ALU.subtract)\
                       .then_inc(am_cent, 1)

            def am_low():
                for k in range(DK):
                    dve.wait_ge(am_h, k + 1)
                    dve.tensor_tensor(am_lo[:, k, :], am_sb[:, k, :], am_hi[:, k, :].bitcast(F32),
                                      ALU.subtract).then_inc(am_l, 1)

            pipeline(dve, step, {0: am_centre, 1: am_low})

        @block.tensor
        def _(pe):
            def product(dst, hi, lo, w_hi, w_lo, cols):
                n = DK
                for k in range(n):
                    pe.matmul(dst, hi[:, k, :], w_hi[:, k, cols], start=(k == 0), stop=False)
                    pe.matmul(dst, hi[:, k, :], w_lo[:, k, cols], start=False, stop=False)
                    mm = pe.matmul(dst, lo[:, k, :], w_hi[:, k, cols], start=False, stop=(k == n - 1))
                return mm

            pe.wait_ge(const_ok, 11)
            pe.wait_ge(ld["wq"], 16)
            for k in range(DK):
                mm = pe.matmul(ps_w0[:], mean_w[:], wq_sb[:, k, :], start=(k == 0), stop=(k == DK - 1))
            mm.then_inc(mean_q, 1)

            def step(p, a, f, g):
                def scores(u):
                    b, rp = u // 2, u % 2
                    if u == 0:
                        pe.wait_ge(qT_hi_ok, nth(1, a, 1))
                        pe.wait_ge(qT_lo_ok, nth(1, a, 1))
                        pe.wait_ge(k_bd_ok, nth(2, a, 2))
                    if not isinstance(a, int) or a >= 1 or u >= 2:
                        pe.wait_ge(diff_ok, nth(U, a, u - 1))
                    elif u == 1:
                        pe.wait_ge(am_cent, 2 * DK)
                    dst = ps_s[:, u % 2, :]
                    q_hi, q_lo = (q[:, b, 2 * rp:2 * rp + 2, :].rearrange("p r q -> p (r q)") for q in (qT_hi, qT_lo))
                    k_hi, k_lo = (k[:, b].rearrange("p h k -> p (h k)") for k in (k_bd_hi, k_bd_lo))
                    pe.matmul(dst, q_hi, k_hi, start=True, stop=False)
                    pe.matmul(dst, q_hi, k_lo, start=False, stop=False)
                    pe.matmul(dst, q_lo, k_hi, start=False, stop=True).then_inc(s_ps, 1)

                def turn(u):
                    pe.wait_ge(diff_ok, nth(U, a, u + 1))
                    if not isinstance(a, int) or a >= 1 or u >= 1:
                        pe.wait_ge(exp_ok, nth(U, a, u))
                    else:
                        pe.wait_ge(am_cent, 2 * DK)
                    for n in range(PAIRS):
                        mm = pe.transpose(ps_d[:, P * n:P * (n + 1)], diff[:, u % 2, P * n:P * (n + 1)], ident[:])
                    mm.then_inc(dT_ps, 1)

                def values(b):
                    pe.wait_ge(exp_ok, nth(U, a, 2 * b + 2))
                    pe.wait_ge(v_bd_ok, nth(4, a, 4))
                    if b == 1 or not isinstance(a, int) or a >= 1:
                        pe.wait_ge(oT_ok, nth(2, a, b))
                    n = REP * BATCH
                    for c in range(PAIRS):
                        pe.matmul(ps_o[32 * c:32 * c + 32, 0:n], v_bd[:, b, c, :], pT[:, b, c, :],
                                  start=True, stop=True)
                    for c in range(PAIRS):
                        mm = pe.matmul(ps_o[32 * c:32 * c + 32, n:2 * n], ones_bd[:], pT[:, b, c, :],
                                       start=True, stop=True)
                    mm.then_inc(o_ps, 1)

                if a is not None:
                    scores(0)
                    scores(1)
                    turn(0)
                if g is not None:
                    pe.wait_ge(zg_ok, nth(2, g, 2))
                    pe.wait_ge(kT_lo_ok, T if p is None else p)
                    for k in range(DK):
                        mm = pe.transpose(ps_t1[:, P * k:P * (k + 1)], zg[:, P * k:P * (k + 1)], ident[:])
                    mm.then_inc(zT_ps, 1)
                if p is not None:
                    if isinstance(p, int) and p == 0:
                        pe.wait_ge(wkv_h, DK)
                        pe.wait_ge(wkv_l, DK)
                    pe.wait_ge(c_hi_ok, nth(1, p, 1))
                    pe.wait_ge(c_lo_ok, nth(1, p, 1))
                    if not isinstance(p, int) or p >= 1:
                        pe.wait_ge(v_st_ok, nth(1, p, 0))
                    product(ps_w1[:, 0:2 * KV], cT_hi, cT_lo, wkv_hi, wkv_lo, slice(0, 2 * KV)).then_inc(kv_ps, 1)
                if g is not None:
                    if isinstance(g, int) and g == 0:
                        pe.wait_ge(b_h, DK)
                        pe.wait_ge(b_l, DK)
                    pe.wait_ge(zT_hi_ok, nth(1, g, 1))
                    pe.wait_ge(zT_lo_ok, nth(1, g, 1))
                    product(ps_w0[:], zT_hi, zT_lo, b_hi, b_lo, slice(0, D)).then_inc(out_ps, 1)
                if a is not None:
                    scores(2)
                    turn(1)
                if p is not None:
                    if isinstance(p, int) and p == 0:
                        pe.wait_ge(wq_l, DK)
                    pe.wait_ge(x_hi_ok, nth(1, p, 1))
                    pe.wait_ge(x_lo_ok, nth(1, p, 1))
                    if g is not None:
                        pe.wait_ge(res_ok, nth(1, g, 1))
                    elif p >= 1:
                        pe.wait_ge(q_rot, nth(2, p, 0))
                    product(ps_w0[:], xT_hi, xT_lo, wq_hi, wq_lo, slice(0, D)).then_inc(q_ps, 1)
                if a is not None:
                    scores(3)
                    turn(2)
                if f is not None:
                    if isinstance(f, int) and f == 0:
                        pe.wait_ge(wo_h, REP)
                        pe.wait_ge(wo_l, REP)
                    pe.wait_ge(oT_hi_ok, nth(1, f, 1))
                    pe.wait_ge(oT_lo_ok, nth(1, f, 1))
                    if p is not None:
                        pe.wait_ge(v_st_ok, nth(1, p, 1))
                    else:
                        pe.wait_ge(zg_ok, nth(2, g, 2))
                    product(ps_w1[:], oT_hi, oT_lo, wo_hi, wo_lo, slice(0, D)).then_inc(y_ps, 1)
                if p is not None:
                    pe.wait_ge(k_rot, nth(3, p, 3))
                    if g is not None:
                        pe.wait_ge(zT_lo_ok, nth(1, g, 1))
                    elif p >= 1:
                        pe.wait_ge(kT_lo_ok, nth(1, p, 0))
                    if isinstance(p, int) and p == 0:
                        pe.wait_ge(const_ok, 14)
                    pe.transpose(ps_t1[:, 0:P], k_r[:], ident[:]).then_inc(kT_ps, 1)
                if a is not None:
                    values(0)
                if f is not None:
                    pe.wait_ge(x2_ok, nth(1, f, 1))
                    pe.wait_ge(qT_lo_ok, T if p is None else p)
                    for k in range(DK):
                        mm = pe.transpose(ps_t0[:, P * k:P * (k + 1)], x2[:, P * k:P * (k + 1)], ident[:])
                    mm.then_inc(x2T_ps, 1)
                if a is not None:
                    turn(3)
                if p is not None:
                    pe.wait_ge(q_r_ok, nth(1, p, 1))
                    if f is not None:
                        pe.wait_ge(x2T_lo_ok, nth(1, f, 1))
                    elif p >= 1:
                        pe.wait_ge(qT_lo_ok, nth(1, p, 0))
                    for k in range(REP):
                        mm = pe.transpose(ps_t0[:, P * k:P * (k + 1)], q_r[:, P * k:P * (k + 1)], ident[:])
                    mm.then_inc(qT_ps, 1)
                if f is not None:
                    if isinstance(f, int) and f == 0:
                        pe.wait_ge(am_h, DK)
                        pe.wait_ge(am_l, DK)
                    pe.wait_ge(x2T_hi_ok, nth(1, f, 1))
                    pe.wait_ge(x2T_lo_ok, nth(1, f, 1))
                    if p is not None:
                        pe.wait_ge(q_rot, nth(2, p, 2))
                    elif g is not None:
                        pe.wait_ge(res_ok, nth(1, g, 1))
                    product(ps_w0[:, 0:HALF], x2T_hi, x2T_lo, am_hi, am_lo, slice(0, HALF)).then_inc(z_ps, 1)
                    product(ps_w1[:, 0:HALF], x2T_hi, x2T_lo, am_hi, am_lo, slice(HALF, AM)).then_inc(z_ps, 1)
                if a is not None:
                    values(1)

            def down_means():
                pe.wait_ge(ld["wr"], 16)
                pe.wait_ge(ld["keys"], 16)
                for k in range(DK):
                    mm = pe.matmul(ps_o[:, E * k:E * (k + 1)], wr_sb[:, P * k:P * (k + 1)], keysT_sb[:],
                                   start=True, stop=True)
                mm.then_inc(route_w, 1)
                pe.wait_ge(route_w, 2)
                pe.wait_ge(ld["am"], 16)
                for dst, c in ((MEAN_A, slice(0, HALF)), (MEAN_B, slice(HALF, AM))):
                    for k in range(DK):
                        mm = pe.matmul(dst, mean_w[:], am_sb[:, k, c], start=(k == 0), stop=(k == DK - 1))
                mm.then_inc(mean_am, 1)

            pipeline(pe, step, {0: down_means})


def kernel(x, ctx_4096, itok_BxS2_0_2047, L0_xattn_Wq, L0_xattn_Wk, L0_xattn_Wv, L0_xattn_Wo,
           L0_ffn_A_w, L0_ffn_B_w, L0_ffn_Wq_w, L0_ffn_keys):
    import concourse.bacc as bacc
    from concourse.bass_utils import run_bass_kernel_spmd

    def rows(w):
        return w.reshape(DK, P, -1).transpose(1, 0, 2)

    def turned(a):
        return a.reshape(T, P, DK, P).transpose(0, 3, 2, 1)

    x, c = np.asarray(x), np.asarray(ctx_4096)
    wo = np.asarray(L0_xattn_Wo).reshape(KVH, REP, HD, D).transpose(0, 2, 1, 3).reshape(KV, REP, D)
    arrays = {
        "x": x.reshape(T, P, D),
        "xT": turned(x.reshape(TOKENS, D)),
        "cT": turned(c.reshape(TOKENS, D)),
        "pos": np.asarray(itok_BxS2_0_2047).reshape(T, P).T,
        "wq": rows(np.asarray(L0_xattn_Wq)),
        "wkv": rows(np.concatenate([np.asarray(L0_xattn_Wk), np.asarray(L0_xattn_Wv)], axis=1)),
        "wo": wo,
        "aT": rows(np.asarray(L0_ffn_A_w).T),
        "wr": np.asarray(L0_ffn_Wq_w),
        "keysT": np.asarray(L0_ffn_keys).T,
        "bT": rows(np.asarray(L0_ffn_B_w).T),
    }
    arrays = {n: np.ascontiguousarray(a) for n, a in arrays.items()}
    nc = bacc.Bacc("TRN2", target_bir_lowering=False, num_devices=1)
    ins = [nc.dram_tensor(n, a.shape, mybir.dt.from_np(a.dtype), kind="ExternalInput").ap()
           for n, a in arrays.items()]
    out = nc.dram_tensor("out", (T, P, D), F32, kind="ExternalOutput").ap()
    build(nc, *ins, out)
    r = run_bass_kernel_spmd(nc, [arrays], core_ids=[0])
    return r.results[0]["out"].reshape(16, BATCH, D)
```

```python
import numpy as np
import concourse.bass as bass
from concourse import mybir
from contextlib import ExitStack

F32 = mybir.dt.float32
F32R = mybir.dt.float32r
I32 = mybir.dt.int32
ALU = mybir.AluOpType
ACT = mybir.ActivationFunctionType
AX = mybir.AxisListType

P = 128
BATCH = 64
D = 512
DK = D // P
HD = 16
KVH = 8
REP = 4
PAIRS = KVH // 2
KV = KVH * HD
E = 64
RANK = 8
TOP = 16
ROUTER = 16
AM = E + D
HALF = AM // 2
E0 = (HALF - E) // RANK
TOKENS = 1024
T = TOKENS // P
U = 4
EPS = 1e-5
SCALE = float(HD) ** -0.5
GATE_SCALE = 32 / TOP
STEPS = 12
WARM = 10
TAKEN = -3.0e38
MAGIC = 1.5 * 2.0 ** 23
TWO_PI = 2 * np.pi
PI_A = float(np.round(TWO_PI * 2 ** 8) / 2 ** 8)
PI_B = float(np.round((TWO_PI - PI_A) * 2 ** 20) / 2 ** 20)
PI_C = float(np.float32(TWO_PI - PI_A - PI_B))
PI_LOW = float(np.nextafter(np.float32(np.pi), np.float32(0)))


def nth(per, t, k):
    return per * t + k


def first(t):
    return isinstance(t, int) and t == 0


def later(t):
    return not first(t)


def build(nc, x, xT, cT, pos, wq, wkv, wo, aT, wr, keysT, bT, out):
    ctx = ExitStack()
    with ctx:
        def sb(name, shape, dt=F32):
            return ctx.enter_context(nc.sbuf_tensor(name, shape, dt))

        def pb(name, shape):
            return ctx.enter_context(nc.psum_tensor(name, shape, F32))

        def sem(name):
            return ctx.enter_context(nc.semaphore(name))

        x_sb = sb("x_sb", [P, T, D])
        xT_in = sb("xT_in", [P, DK, P])
        cT_in = sb("cT_in", [P, DK, P])
        wq_sb = sb("wq_sb", [P, DK, D])
        wkv_sb = sb("wkv_sb", [P, DK, 2 * KV])
        wo_sb = sb("wo_sb", [P, REP, D])
        am_sb = sb("am_sb", [P, DK, AM])
        wr_sb = sb("wr_sb", [ROUTER, D])
        keysT_sb = sb("keysT_sb", [ROUTER, E])
        pos_sb = sb("pos_sb", [P, T], I32)
        wq_hi, wq_lo = sb("wq_hi", [P, DK, D], F32R), sb("wq_lo", [P, DK, D], F32R)
        wkv_hi, wkv_lo = sb("wkv_hi", [P, DK, 2 * KV], F32R), sb("wkv_lo", [P, DK, 2 * KV], F32R)
        wo_hi, wo_lo = sb("wo_hi", [P, REP, D], F32R), sb("wo_lo", [P, REP, D], F32R)
        am_hi, am_lo = sb("am_hi", [P, DK, AM], F32R), sb("am_lo", [P, DK, AM], F32R)
        b_hi, b_lo = sb("b_hi", [P, DK, D], F32R), sb("b_lo", [P, DK, D], F32R)
        b_sb = wq_sb
        warm = sb("warm", [P, D], mybir.dt.bfloat16)
        ident = sb("ident", [P, P])
        mean_w = sb("mean_w", [P, P])
        head_mask = sb("head_mask", [P, KVH])
        freq = sb("freq", [P, HD // 2])
        half_pi = sb("half_pi", [P, 1])
        neg_half = sb("neg_half", [P, 1])
        pos_f = sb("pos_f", [P, T])
        ang = sb("ang", [P, T, HD // 2])
        turns = sb("turns", [P, T, HD // 2])
        rem = sb("rem", [P, 3, T, HD // 2])
        abs_r = sb("abs_r", [P, T, HD // 2])
        cs = sb("cs", [P, T, 2 * HD])
        cs_q = sb("cs_q", [P, 2 * HD])
        xT_hi, xT_lo = sb("xT_hi", [P, DK, P], F32R), sb("xT_lo", [P, DK, P], F32R)
        cT_hi, cT_lo = sb("cT_hi", [P, DK, P], F32R), sb("cT_lo", [P, DK, P], F32R)
        bn1, mv1, ve1, rstd1 = sb("bn1", [P, 6]), sb("mv1", [P, 2]), sb("ve1", [P, 1]), sb("rstd1", [P, 1])
        q_a, q_b, q_r = sb("q_a", [P, D]), sb("q_b", [P, D]), sb("q_r", [P, D])
        k_a, k_b, k_r = sb("k_a", [P, KV]), sb("k_b", [P, KV]), sb("k_r", [P, KV])
        v_st = sb("v_st", [P, KV])
        kT_hi, kT_lo = sb("kT_hi", [P, P], F32R), sb("kT_lo", [P, P], F32R)
        qT_hi, qT_lo = sb("qT_hi", [P, 2, REP, BATCH], F32R), sb("qT_lo", [P, 2, REP, BATCH], F32R)
        k_bd_hi = sb("k_bd_hi", [P, 2, KVH, BATCH], F32R)
        k_bd_lo = sb("k_bd_lo", [P, 2, KVH, BATCH], F32R)
        v_bd = sb("v_bd", [P, 2, PAIRS, 2 * HD])
        neg_top = sb("neg_top", [P, U, KVH])
        e_un = sb("e_un", [P, 2, D])
        sums = sb("sums", [P, U, KVH])
        inv = sb("inv", [P, U, KVH])
        prob = sb("prob", [P, 2, D])
        pT = sb("pT", [P, 2, PAIRS, REP * BATCH])
        oT_hi = sb("oT_hi", [P, REP, 2, BATCH], F32R)
        oT_lo = sb("oT_lo", [P, REP, 2, BATCH], F32R)
        bn2, mv2, ve2, rstd2 = sb("bn2", [P, 6]), sb("mv2", [P, 2]), sb("ve2", [P, 1]), sb("rstd2", [P, 1])
        x2 = sb("x2", [P, D])
        x2T_hi, x2T_lo = sb("x2T_hi", [P, DK, P], F32R), sb("x2T_lo", [P, DK, P], F32R)
        s_sb, s_a, s_b = sb("s_sb", [P, E]), sb("s_a", [P, E]), sb("s_b", [P, E])
        top_a, top_b = sb("top_a", [P, 8]), sb("top_b", [P, 8])
        neg_max, e_sum, e_inv, g_scale = (sb(n, [P, 1]) for n in ("neg_max", "e_sum", "e_inv", "g_scale"))
        e_sb, e_top, gate = sb("e_sb", [P, E]), sb("e_top", [P, E]), sb("gate", [P, E])
        zg = sb("zg", [P, D])
        zT_hi, zT_lo = sb("zT_hi", [P, DK, P], F32R), sb("zT_lo", [P, DK, P], F32R)
        res = sb("res", [P, D])

        ps_s = pb("ps_s", [P, 2, D])
        ps_d = pb("ps_d", [P, D])
        ps_o = pb("ps_o", [P, 2, REP * BATCH])
        ps_w0, ps_w1 = pb("ps_w0", [P, D]), pb("ps_w1", [P, D])
        ps_t0, ps_t1 = pb("ps_t0", [P, D]), pb("ps_t1", [P, D])
        MEAN_A, MEAN_B = ps_w0[:, 0:HALF], ps_t0[:, 0:HALF]
        ROUTE = ps_o[:].rearrange("p b n -> p (b n)")[:, 0:DK * E]

        ld = {n: sem("ld_" + n) for n in ("c", "x", "xnat0", "xnat", "pos", "wkv", "wo", "am",
                                           "wr", "keys", "b")}
        ld_wq = [sem(f"ld_wq{k}") for k in range(DK)]
        warm_ok = sem("warm_ok")
        const_ok = sem("const_ok")
        mask_step = sem("mask_step")
        rope_step = sem("rope_step")
        cs_ok = sem("cs_ok")
        mean_q = sem("mean_q")
        wq_cent = sem("wq_cent")
        wq_h = sem("wq_h")
        wq_l0, wq_l = sem("wq_l0"), sem("wq_l")
        wkv_h, wkv_l = sem("wkv_h"), sem("wkv_l")
        wo_h, wo_l = sem("wo_h"), sem("wo_l")
        route_w = sem("route_w")
        mean_am = sem("mean_am")
        am_cent = sem("am_cent")
        am_h, am_l = sem("am_h"), sem("am_l")
        b_h, b_l, b_l2 = sem("b_h"), sem("b_l"), sem("b_l2")
        c_hi_ok, c_lo_ok, x_hi_ok, x_lo_ok = sem("c_hi_ok"), sem("c_lo_ok"), sem("x_hi_ok"), sem("x_lo_ok")
        stat1 = sem("stat1")
        rstd1_ok = sem("rstd1_ok")
        cs_q_ok = sem("cs_q_ok")
        kv_ps, q_ps = sem("kv_ps"), sem("q_ps")
        k_rot = sem("k_rot")
        v_st_ok = sem("v_st_ok")
        q_rot = sem("q_rot")
        q_r_ok = sem("q_r_ok")
        kT_ps, qT_ps = sem("kT_ps"), sem("qT_ps")
        kT_hi_ok, kT_lo_ok = sem("kT_hi_ok"), sem("kT_lo_ok")
        qT_hi_ok, qT_lo_ok = sem("qT_hi_ok"), sem("qT_lo_ok")
        k_bd_ok = sem("k_bd_ok")
        v_bd_ok = sem("v_bd_ok")
        s_ps = sem("s_ps")
        max_ok = sem("max_ok")
        exp_ok = sem("exp_ok")
        inv_ok = sem("inv_ok")
        prob_ok = sem("prob_ok")
        pT_ps = sem("pT_ps")
        pT_ok = sem("pT_ok")
        o_ps = sem("o_ps")
        oT_hi_ok, oT_lo_ok = sem("oT_hi_ok"), sem("oT_lo_ok")
        y_ps = sem("y_ps")
        x2_ok = sem("x2_ok")
        stat2 = sem("stat2")
        rstd2_ok = sem("rstd2_ok")
        x2T_ps, x2T_hi_ok, x2T_lo_ok = sem("x2T_ps"), sem("x2T_hi_ok"), sem("x2T_lo_ok")
        z_ps = sem("z_ps")
        s_ok = sem("s_ok")
        top_step = sem("top_step")
        e_ok = sem("e_ok")
        zg_ok = sem("zg_ok")
        zT_ps, zT_hi_ok, zT_lo_ok = sem("zT_ps"), sem("zT_hi_ok"), sem("zT_lo_ok")
        out_ps = sem("out_ps")
        res_ok = sem("res_ok")
        stored = sem("stored")

        block = ctx.enter_context(nc.Block())

        def pipeline(eng, step):
            def tiles(i):
                return [t if 0 <= t < T else None for t in (i + 1, i, i - 1, i - 2)]
            for i in (-1, 0, 1, 2):
                step(*tiles(i))
            with eng.Fori(3, T - 1) as i:
                step(i + 1, i, i - 1, i - 2)
            for i in range(T - 1, T + 2):
                step(*tiles(i))

        @block.sync
        def _(sp):
            def load(dst, src, name):
                sp.dma_start(dst, src).then_inc(ld[name], 16)

            for k in range(DK):
                sp.dma_start(wq_sb[:, k, :], wq[:, k, :]).then_inc(ld_wq[k], 16)
            load(wo_sb[:], wo, "wo")
            load(am_sb[:, :, E:AM], aT, "am")
            load(x_sb[:, 1:T, :], x[1:T].rearrange("t p d -> p t d"), "xnat")

            def load_tile(t):
                sp.wait_ge(c_hi_ok, t)
                sp.wait_ge(c_lo_ok, t)
                load(cT_in[:], cT[t], "c")
                sp.wait_ge(x_hi_ok, t)
                sp.wait_ge(x_lo_ok, t)
                load(xT_in[:], xT[t], "x")

            def store_tile(t):
                sp.wait_ge(res_ok, t + 1)
                sp.dma_start(out[t], res[:]).then_inc(stored, 16)

            load_tile(1)
            sp.wait_ge(wq_h, DK)
            sp.wait_ge(wq_l0, 1)
            sp.wait_ge(wq_l, DK - 1)
            load(b_sb[:], bT, "b")
            with sp.Fori(2, 4) as t:
                load_tile(t)
            with sp.Fori(4, T) as t:
                load_tile(t)
                store_tile(t - 4)
            with sp.Fori(T - 4, T) as t:
                store_tile(t)
            sp.wait_ge(stored, 16 * T)

        @block.gpsimd
        def _(pool):
            pool.memset(mean_w[:], 1.0 / D).then_inc(const_ok, 1)
            for j in range(HD // 2):
                f = np.float32(1.0) / np.float32(10000.0) ** np.float32(2 * j / HD)
                pool.memset(freq[:, j:j + 1], float(f)).then_inc(const_ok, 1)
            pool.memset(half_pi[:], float(np.pi / 2)).then_inc(const_ok, 1)
            pool.memset(neg_half[:], -0.5).then_inc(const_ok, 1)
            pool.memset(v_bd[:], 0.0).then_inc(mask_step, 1)
            pool.memset(head_mask[:], SCALE).then_inc(mask_step, 1)
            pool.memset(ident[:], 0.0).then_inc(mask_step, 1)
            pool.wait_ge(mask_step, 3)
            pool.affine_select(out=ident[:], in_=ident[:], compare_op=ALU.not_equal, fill=1.0, base=0,
                               pattern=[[-1, P]], channel_multiplier=1).then_inc(const_ok, 1)
            pool.affine_select(out=head_mask[:], in_=head_mask[:], compare_op=ALU.is_ge, fill=0.0, base=0,
                               pattern=[[-HD, KVH]], channel_multiplier=1).then_inc(mask_step, 1)
            pool.wait_ge(mask_step, 4)
            pool.affine_select(out=head_mask[:], in_=head_mask[:], compare_op=ALU.is_ge, fill=0.0, base=HD - 1,
                               pattern=[[HD, KVH]], channel_multiplier=-1).then_inc(const_ok, 1)

            def split_lo(lo, raw, hi, high, low, k):
                pool.wait_ge(high, k + 1)
                pool.tensor_tensor(lo[:, k, :], raw[:, k, :], hi[:, k, :].bitcast(F32),
                                   ALU.subtract).then_inc(low, 1)

            def step(p, a, f, g):
                def normalise(u):
                    pool.wait_ge(inv_ok, nth(U, a, u + 1))
                    if later(a) or u >= 2:
                        pool.wait_ge(pT_ps, nth(U, a, u - 1))
                    pool.tensor_tensor(prob[:, u % 2, :].rearrange("p (h k) -> p h k", h=KVH),
                                       e_un[:, u % 2, :].rearrange("p (h k) -> p h k", h=KVH),
                                       inv[:, u, :].unsqueeze(2).broadcast_to([P, KVH, BATCH]),
                                       ALU.mult).then_inc(prob_ok, 1)

                if p is not None:
                    pool.wait_ge(c_hi_ok, nth(1, p, 1))
                    if later(p):
                        pool.wait_ge(kv_ps, nth(1, p, 0))
                    pool.tensor_tensor(cT_lo[:], cT_in[:], cT_hi[:].bitcast(F32), ALU.subtract).then_inc(c_lo_ok, 1)
                if first(a):
                    for k in range(2):
                        split_lo(wo_lo, wo_sb, wo_hi, wo_h, wo_l, k)
                if a is not None:
                    normalise(0)
                    normalise(1)
                if p is not None:
                    pool.wait_ge(x_hi_ok, nth(1, p, 1))
                    if later(p):
                        pool.wait_ge(q_ps, nth(1, p, 0))
                    pool.tensor_tensor(xT_lo[:], xT_in[:], xT_hi[:].bitcast(F32), ALU.subtract).then_inc(x_lo_ok, 1)
                    if first(p):
                        split_lo(wq_lo, wq_sb, wq_hi, wq_h, wq_l0, 0)
                    pool.wait_ge(stat1, nth(3, p, 3))
                    if later(p):
                        pool.wait_ge(cs_q_ok, nth(1, p, 0))
                    pool.tensor_tensor(rstd1[:], ve1[:], neg_half[:], ALU.pow).then_inc(rstd1_ok, 1)

                def k_blocks(n):
                    bd, kT, ok = ((k_bd_hi, kT_hi, kT_hi_ok), (k_bd_lo, kT_lo, kT_lo_ok))[n]
                    pool.wait_ge(ok, nth(1, p, 1))
                    if a is not None:
                        pool.wait_ge(s_ps, nth(U, a, U))
                    pool.tensor_tensor(
                        bd[:],
                        kT[:].bitcast(F32).rearrange("p (b q) -> p b q", b=2).unsqueeze(2)
                        .broadcast_to([P, 2, KVH, BATCH]),
                        head_mask[:].unsqueeze(1).unsqueeze(3).broadcast_to([P, 2, KVH, BATCH]),
                        ALU.mult).then_inc(k_bd_ok, 1)

                if p is not None:
                    k_blocks(0)
                if a is not None:
                    normalise(2)
                    normalise(3)
                if f is not None:
                    pool.wait_ge(stat2, nth(3, f, 3))
                    if later(f):
                        pool.wait_ge(top_step, nth(STEPS, f, 0))
                        pool.wait_ge(e_ok, nth(1, f, 0))
                    pool.tensor_tensor(rstd2[:], ve2[:], neg_half[:], ALU.pow).then_inc(rstd2_ok, 1)
                if p is not None:
                    k_blocks(1)
                if first(a):
                    for k in range(2, REP):
                        split_lo(wo_lo, wo_sb, wo_hi, wo_h, wo_l, k)
                if first(f):
                    for k in range(2):
                        split_lo(b_lo, b_sb, b_hi, b_h, b_l, k)

            pipeline(pool, step)

        @block.scalar
        def _(act):
            for dst, src, name in ((pos_sb[:], pos, "pos"), (wkv_sb[:], wkv, "wkv"), (cT_in[:], cT[0], "c"),
                                   (xT_in[:], xT[0], "x"), (x_sb[:, 0, :], x[0], "xnat0"),
                                   (wr_sb[:], wr, "wr"), (keysT_sb[:], keysT, "keys")):
                act.dma_start(dst, src).then_inc(ld[name], 16)
            act.wait_ge(const_ok, 10)
            act.wait_ge(rope_step, 9)
            act.activation(cs[:, :, 24:32], rem[:, 2], ACT.Sin).then_inc(cs_ok, 1)
            act.activation(cs[:, :, 16:24], rem[:, 2], ACT.Sin, scale=-1.0).then_inc(cs_ok, 1)
            for c in range(2):
                act.activation(cs[:, :, 8 * c:8 * c + 8], abs_r[:], ACT.Sin, scale=-1.0,
                               bias=half_pi[:]).then_inc(cs_ok, 1)
            act.wait_ge(ld["wkv"], 16)
            act.activation(wkv_hi[:], wkv_sb[:], ACT.Copy).then_inc(wkv_h, 1)

            def step(p, a, f, g):
                def exps(u):
                    act.wait_ge(max_ok, nth(U, a, u + 1))
                    if later(a) or u >= 2:
                        act.wait_ge(prob_ok, nth(U, a, u - 1))
                    for h in range(KVH):
                        c = slice(BATCH * h, BATCH * (h + 1))
                        last = act.activation(e_un[:, u % 2, c], ps_s[:, u % 2, c], ACT.Exp,
                                              bias=neg_top[:, u, h:h + 1], accum_out=sums[:, u, h:h + 1])
                    last.then_inc(exp_ok, 1)

                def turned(u):
                    act.wait_ge(pT_ps, nth(U, a, u + 1))
                    b, rp = u // 2, u % 2
                    if later(a):
                        act.wait_ge(o_ps, nth(2, a, b - 1))
                    act.activation(pT[:, b, :, P * rp:P * (rp + 1)],
                                   ps_d[:].rearrange("p (g q) -> p g q", g=PAIRS), ACT.Copy).then_inc(pT_ok, 1)

                def o_high(t, b):
                    act.wait_ge(o_ps, nth(2, t, b + 1))
                    if later(t):
                        act.wait_ge(y_ps, nth(1, t, 0))
                    act.activation(oT_hi[:, :, b, :], ps_o[:, b, :].rearrange("p (r q) -> p r q", r=REP),
                                   ACT.Copy).then_inc(oT_hi_ok, 1)

                def x_high():
                    act.wait_ge(ld["x"], nth(16, p, 16))
                    if later(p):
                        act.wait_ge(q_ps, nth(1, p, 0))
                        act.wait_ge(x_lo_ok, nth(1, p, 0))
                    act.activation(xT_hi[:], xT_in[:], ACT.Copy).then_inc(x_hi_ok, 1)

                if p is not None:
                    act.wait_ge(ld["c"], nth(16, p, 16))
                    if later(p):
                        act.wait_ge(kv_ps, nth(1, p, 0))
                        act.wait_ge(c_lo_ok, nth(1, p, 0))
                    act.activation(cT_hi[:], cT_in[:], ACT.Copy).then_inc(c_hi_ok, 1)
                if first(p):
                    x_high()
                    for k in range(DK):
                        act.wait_ge(wq_cent, k + 1)
                        act.activation(wq_hi[:, k, :], wq_sb[:, k, :], ACT.Copy).then_inc(wq_h, 1)
                    act.wait_ge(route_w, 1)
                    act.activation(am_sb[:, :, 0:E], ROUTE.rearrange("p (k e) -> p k e", k=DK),
                                   ACT.Copy).then_inc(route_w, 1)
                if g is not None:
                    act.wait_ge(zT_ps, nth(1, g, 1))
                    act.activation(zT_hi[:], ps_t1[:].rearrange("p (k q) -> p k q", k=DK), ACT.Copy)\
                       .then_inc(zT_hi_ok, 1)
                if a is not None:
                    exps(0)
                if f is not None:
                    o_high(f, 1)
                if a is not None:
                    act.wait_ge(v_st_ok, nth(1, a, 1))
                    if later(a):
                        act.wait_ge(o_ps, nth(2, a, 0))
                    else:
                        act.wait_ge(mask_step, 3)
                    for b in range(2):
                        for h in range(2):
                            act.activation(
                                v_bd[BATCH * h:BATCH * (h + 1), b, :, HD * h:HD * (h + 1)],
                                v_st[BATCH * b:BATCH * (b + 1), :]
                                .rearrange("p (g h d) -> p g h d", g=PAIRS, h=2)[:, :, h, :],
                                ACT.Copy).then_inc(v_bd_ok, 1)
                if p is not None:
                    act.wait_ge(k_rot, nth(3, p, 2))
                    act.wait_ge(kv_ps, nth(1, p, 1))
                    if a is not None:
                        act.wait_ge(v_bd_ok, nth(4, a, 4))
                    act.activation(v_st[:], ps_w1[:, KV:2 * KV], ACT.Copy).then_inc(v_st_ok, 1)
                if a is not None:
                    exps(1)
                if p is not None:
                    act.wait_ge(kT_ps, nth(1, p, 1))
                    if later(p):
                        act.wait_ge(k_bd_ok, nth(2, p, 0))
                    act.activation(kT_hi[:], ps_t1[:, 0:P], ACT.Copy).then_inc(kT_hi_ok, 1)
                if a is not None:
                    turned(0)
                if first(p):
                    act.wait_ge(ld["wo"], 16)
                    for k in range(REP):
                        act.activation(wo_hi[:, k, :], wo_sb[:, k, :], ACT.Copy).then_inc(wo_h, 1)
                elif p is not None:
                    x_high()
                if a is not None:
                    exps(2)
                    exps(3)
                    turned(1)
                if f is not None:
                    act.wait_ge(x2T_ps, nth(1, f, 1))
                    if later(f):
                        act.wait_ge(z_ps, nth(2, f, 0))
                    act.activation(x2T_hi[:], ps_t0[:].rearrange("p (k q) -> p k q", k=DK), ACT.Copy)\
                       .then_inc(x2T_hi_ok, 1)
                if a is not None:
                    turned(2)
                    o_high(a, 0)
                    turned(3)
                if first(a):
                    for k in range(DK):
                        act.wait_ge(am_cent, DK + k + 1)
                        act.activation(am_hi[:, k, :], am_sb[:, k, :], ACT.Copy).then_inc(am_h, 1)
                if f is not None:
                    act.wait_ge(z_ps, nth(2, f, 1))
                    if later(f):
                        act.wait_ge(top_step, nth(STEPS, f, 0))
                    act.activation(s_sb[:], ps_w1[:, 0:E], ACT.Copy).then_inc(s_ok, 1)
                if p is not None:
                    act.wait_ge(qT_ps, nth(1, p, 1))
                    if a is not None:
                        act.wait_ge(s_ps, nth(U, a, U))
                    act.activation(qT_hi[:].rearrange("p b r q -> p r b q"),
                                   ps_t0[:].rearrange("p (r b q) -> p r b q", r=REP, b=2),
                                   ACT.Copy).then_inc(qT_hi_ok, 1)
                if f is not None:
                    act.wait_ge(s_ok, nth(1, f, 1))
                    act.wait_ge(rstd2_ok, nth(1, f, 1))
                    act.wait_ge(top_step, nth(STEPS, f, 3))
                    act.activation(e_sb[:], s_sb[:], ACT.Exp, scale=rstd2[:], bias=neg_max[:]).then_inc(e_ok, 1)
                if first(f):
                    act.wait_ge(ld["b"], 16)
                    for k in range(DK):
                        act.activation(b_hi[:, k, :], b_sb[:, k, :], ACT.Copy).then_inc(b_h, 1)

            pipeline(act, step)

        @block.vector
        def _(dve):
            dve.memset(warm[:], 0.0).then_inc(warm_ok, 1)
            dve.wait_ge(ld["pos"], 16)
            dve.tensor_copy(pos_f[:], pos_sb[:]).then_inc(rope_step, 1)
            dve.wait_ge(rope_step, 1)
            dve.wait_ge(const_ok, 9)
            J = HD // 2
            dve.tensor_tensor(ang[:], pos_f[:].unsqueeze(2).broadcast_to([P, T, J]),
                              freq[:].unsqueeze(1).broadcast_to([P, T, J]), ALU.mult).then_inc(rope_step, 1)
            dve.wait_ge(rope_step, 2)
            dve.tensor_scalar(turns[:], ang[:], float(1 / TWO_PI), MAGIC, ALU.mult, ALU.add).then_inc(rope_step, 1)
            dve.wait_ge(rope_step, 3)
            dve.tensor_scalar(turns[:], turns[:], MAGIC, None, ALU.subtract).then_inc(rope_step, 1)
            dve.wait_ge(rope_step, 4)
            for n, (part, src) in enumerate(((PI_A, ang[:]), (PI_B, rem[:, 0]), (PI_C, rem[:, 1]))):
                dve.scalar_tensor_tensor(rem[:, n], turns[:], -part, src, ALU.mult, ALU.add)\
                   .then_inc(rope_step, 1)
                dve.wait_ge(rope_step, 5 + n)
            dve.tensor_scalar(rem[:, 2], rem[:, 2], PI_LOW, -PI_LOW, ALU.min, ALU.max).then_inc(rope_step, 1)
            dve.wait_ge(rope_step, 8)
            dve.scalar_tensor_tensor(abs_r[:], rem[:, 2], -1.0, rem[:, 2], ALU.mult, ALU.max)\
               .then_inc(rope_step, 1)
            dve.wait_ge(wkv_h, 1)
            dve.tensor_tensor(wkv_lo[:], wkv_sb[:], wkv_hi[:].bitcast(F32), ALU.subtract).then_inc(wkv_l, 1)

            def split_lo(lo, raw, hi, high, low, k):
                dve.wait_ge(high, k + 1)
                dve.tensor_tensor(lo[:, k, :], raw[:, k, :], hi[:, k, :].bitcast(F32), ALU.subtract)\
                   .then_inc(low, 1)

            def step(p, a, f, g):
                def top(u):
                    dve.wait_ge(s_ps, nth(U, a, u + 1))
                    dve.tensor_reduce(neg_top[:, u, :], ps_s[:, u % 2, :].rearrange("p (h k) -> p h k", h=KVH),
                                      AX.X, ALU.max, negate=True).then_inc(max_ok, 1)

                def invert(u):
                    dve.wait_ge(exp_ok, nth(U, a, u + 1))
                    dve.reciprocal(inv[:, u, :], sums[:, u, :]).then_inc(inv_ok, 1)

                def o_low(t, b):
                    dve.wait_ge(oT_hi_ok, nth(2, t, b + 1))
                    dve.tensor_tensor(oT_lo[:, :, b, :], ps_o[:, b, :].rearrange("p (r q) -> p r q", r=REP),
                                      oT_hi[:, :, b, :].bitcast(F32), ALU.subtract).then_inc(oT_lo_ok, 1)

                if a is not None:
                    top(0)
                    top(1)
                if g is not None:
                    dve.wait_ge(zT_hi_ok, nth(1, g, 1))
                    dve.tensor_tensor(zT_lo[:], ps_t1[:].rearrange("p (k q) -> p k q", k=DK),
                                      zT_hi[:].bitcast(F32), ALU.subtract).then_inc(zT_lo_ok, 1)
                if first(p):
                    dve.wait_ge(mean_q, 1)
                    for k in range(DK):
                        dve.tensor_tensor(wq_sb[:, k, :], wq_sb[:, k, :], ps_w0[:], ALU.subtract)\
                           .then_inc(wq_cent, 1)
                if p is not None:
                    if first(p):
                        dve.wait_ge(cs_ok, 4)
                    dve.wait_ge(kv_ps, nth(1, p, 1))
                    k_ps = ps_w1[:, 0:KV].rearrange("p (h s j) -> p h s j", h=KVH, s=2)

                    def table(t, at, n):
                        return t[:, at:at + HD].rearrange("p (s j) -> p s j", s=2).unsqueeze(1)\
                            .broadcast_to([P, n, 2, J])

                    dve.tensor_tensor(k_a[:].rearrange("p (h s j) -> p h s j", h=KVH, s=2), k_ps,
                                      table(cs[:, p, :], 0, KVH), ALU.mult).then_inc(k_rot, 1)
                    dve.tensor_tensor(k_b[:].rearrange("p (h s j) -> p h s j", h=KVH, s=2), k_ps[:, :, ::-1, :],
                                      table(cs[:, p, :], HD, KVH), ALU.mult).then_inc(k_rot, 1)
                    dve.wait_ge(k_rot, nth(3, p, 2))
                    if later(p):
                        dve.wait_ge(kT_ps, nth(1, p, 0))
                    dve.tensor_tensor(k_r[:], k_a[:], k_b[:], ALU.add).then_inc(k_rot, 1)
                if first(p):
                    for k in range(1, DK):
                        split_lo(wq_lo, wq_sb, wq_hi, wq_h, wq_l, k)
                if a is not None:
                    invert(0)
                if f is not None:
                    o_low(f, 1)
                if p is not None:
                    dve.wait_ge(ld["xnat0" if first(p) else "xnat"], 16)
                    dve.bn_stats(bn1[:], x_sb[:, p, :]).then_inc(stat1, 1)

                def am_centre(cols, mean):
                    dve.wait_ge(mean_am, 1)
                    for k in range(DK):
                        dve.tensor_tensor(am_sb[:, k, cols], am_sb[:, k, cols], mean, ALU.subtract)\
                           .then_inc(am_cent, 1)

                if first(a):
                    am_centre(slice(0, HALF), MEAN_A)
                if g is not None:
                    dve.wait_ge(out_ps, nth(1, g, 1))
                    if later(g):
                        dve.wait_ge(stored, nth(16, g, 0))
                    dve.tensor_tensor(res[:], ps_w0[:], x2[:], ALU.add).then_inc(res_ok, 1)
                if a is not None:
                    top(2)
                    invert(1)
                if p is not None:
                    dve.wait_ge(stat1, nth(3, p, 1))
                    dve.wait_ge(kT_hi_ok, nth(1, p, 1))
                    if later(p):
                        dve.wait_ge(k_bd_ok, nth(2, p, 0))
                    dve.tensor_tensor(kT_lo[:], ps_t1[:, 0:P], kT_hi[:].bitcast(F32), ALU.subtract)\
                       .then_inc(kT_lo_ok, 1)
                    dve.bn_aggr(mv1[:], bn1[:]).then_inc(stat1, 1)
                    dve.wait_ge(stat1, nth(3, p, 2))
                    if later(p):
                        dve.wait_ge(rstd1_ok, nth(1, p, 0))
                    dve.tensor_scalar_add(ve1[:], mv1[:, 1:2], EPS).then_inc(stat1, 1)
                if f is not None:
                    dve.wait_ge(y_ps, nth(1, f, 1))
                    if later(f):
                        dve.wait_ge(x2T_ps, nth(1, f, 0))
                        dve.wait_ge(res_ok, nth(1, f, 0))
                    dve.tensor_tensor(x2[:], ps_w1[:], x_sb[:, f, :], ALU.add).then_inc(x2_ok, 1)
                if a is not None:
                    top(3)
                    invert(2)
                if f is not None:
                    dve.wait_ge(x2_ok, nth(1, f, 1))
                    dve.bn_stats(bn2[:], x2[:]).then_inc(stat2, 1)
                if first(a):
                    am_centre(slice(HALF, AM), MEAN_B)
                if p is not None:
                    dve.wait_ge(rstd1_ok, nth(1, p, 1))
                    if later(p):
                        dve.wait_ge(q_rot, nth(2, p, 0))
                    if f is not None:
                        dve.wait_ge(stat2, nth(3, f, 1))
                    dve.tensor_scalar_mul(cs_q[:], cs[:, p, :], rstd1[:]).then_inc(cs_q_ok, 1)
                elif f is not None:
                    dve.wait_ge(stat2, nth(3, f, 1))
                if f is not None:
                    dve.bn_aggr(mv2[:], bn2[:]).then_inc(stat2, 1)
                    dve.wait_ge(stat2, nth(3, f, 2))
                    if later(f):
                        dve.wait_ge(rstd2_ok, nth(1, f, 0))
                    dve.tensor_scalar_add(ve2[:], mv2[:, 1:2], EPS).then_inc(stat2, 1)
                if first(f):
                    for k in range(DK):
                        split_lo(am_lo, am_sb, am_hi, am_h, am_l, k)
                if a is not None:
                    invert(3)
                if f is not None:
                    dve.wait_ge(x2T_hi_ok, nth(1, f, 1))
                    dve.tensor_tensor(x2T_lo[:], ps_t0[:].rearrange("p (k q) -> p k q", k=DK),
                                      x2T_hi[:].bitcast(F32), ALU.subtract).then_inc(x2T_lo_ok, 1)
                if p is not None:
                    dve.wait_ge(q_ps, nth(1, p, 1))
                    dve.wait_ge(cs_q_ok, nth(1, p, 1))
                    if later(p):
                        dve.wait_ge(q_r_ok, nth(1, p, 0))
                    H = REP * KVH
                    w = ps_w0[:].rearrange("p (h s j) -> p h s j", h=H, s=2)
                    dve.tensor_tensor(q_a[:].rearrange("p (h s j) -> p h s j", h=H, s=2), w,
                                      table(cs_q, 0, H), ALU.mult).then_inc(q_rot, 1)
                    dve.tensor_tensor(q_b[:].rearrange("p (h s j) -> p h s j", h=H, s=2), w[:, :, ::-1, :],
                                      table(cs_q, HD, H), ALU.mult).then_inc(q_rot, 1)
                    dve.wait_ge(q_rot, nth(2, p, 2))
                    if later(p):
                        dve.wait_ge(qT_ps, nth(1, p, 0))
                    dve.tensor_tensor(q_r[:].rearrange("p (r k d) -> p k r d", r=REP, k=KVH),
                                      q_a[:].rearrange("p (k r d) -> p k r d", r=REP, k=KVH),
                                      q_b[:].rearrange("p (k r d) -> p k r d", r=REP, k=KVH),
                                      ALU.add).then_inc(q_r_ok, 1)
                if a is not None:
                    o_low(a, 0)

                def q_low():
                    dve.wait_ge(qT_hi_ok, nth(1, p, 1))
                    dve.tensor_tensor(qT_lo[:].rearrange("p b r q -> p r b q"),
                                      ps_t0[:].rearrange("p (r b q) -> p r b q", r=REP, b=2),
                                      qT_hi[:].bitcast(F32).rearrange("p b r q -> p r b q"),
                                      ALU.subtract).then_inc(qT_lo_ok, 1)

                if f is None and p is not None:
                    q_low()
                if f is not None:
                    dve.wait_ge(s_ok, nth(1, f, 1))
                    dve.memset(e_top[:, 0:1], 0.0).then_inc(top_step, 1)
                    dve.max(top_a[:], s_sb[:]).then_inc(top_step, 1)
                    dve.wait_ge(rstd2_ok, nth(1, f, 1))
                    dve.wait_ge(top_step, nth(STEPS, f, 2))
                    dve.tensor_scalar(neg_max[:], top_a[:, 0:1], rstd2[:], -1.0, ALU.mult, ALU.mult)\
                       .then_inc(top_step, 1)
                    dve.match_replace(s_a[:], top_a[:], s_sb[:], TAKEN).then_inc(top_step, 1)
                    dve.wait_ge(top_step, nth(STEPS, f, 4))
                    dve.memset(e_top[:, 1:2], 0.0).then_inc(top_step, 1)
                    dve.max(top_b[:], s_a[:]).then_inc(top_step, 1)
                    dve.wait_ge(top_step, nth(STEPS, f, 6))
                    dve.memset(e_top[:, 2:3], 0.0).then_inc(top_step, 1)
                    dve.match_replace(s_b[:], top_b[:], s_a[:], TAKEN).then_inc(top_step, 1)
                    if p is not None:
                        q_low()
                    dve.wait_ge(top_step, nth(STEPS, f, 8))
                    dve.wait_ge(e_ok, nth(1, f, 1))
                    dve.scalar_tensor_tensor(e_top[:], s_b[:], TAKEN, e_sb[:], ALU.is_equal, ALU.mult,
                                             accum_out=e_sum[:]).then_inc(top_step, 1)
                    dve.wait_ge(top_step, nth(STEPS, f, 9))
                    dve.reciprocal(e_inv[:], e_sum[:]).then_inc(top_step, 1)
                    dve.wait_ge(top_step, nth(STEPS, f, 10))
                    dve.tensor_scalar(g_scale[:], e_inv[:], rstd2[:], GATE_SCALE, ALU.mult, ALU.mult)\
                       .then_inc(top_step, 1)
                    dve.wait_ge(top_step, nth(STEPS, f, 11))
                    dve.tensor_scalar_mul(gate[:], e_top[:], g_scale[:]).then_inc(top_step, 1)
                    dve.wait_ge(top_step, nth(STEPS, f, 12))
                    if later(f):
                        dve.wait_ge(zT_ps, nth(1, f, 0))
                    n0 = E0 * RANK
                    dve.tensor_tensor(zg[:, 0:n0].rearrange("p (e r) -> p e r", r=RANK),
                                      ps_w1[:, E:HALF].rearrange("p (e r) -> p e r", r=RANK),
                                      gate[:, 0:E0].unsqueeze(2).broadcast_to([P, E0, RANK]),
                                      ALU.mult).then_inc(zg_ok, 1)
                    dve.wait_ge(z_ps, nth(2, f, 2))
                    dve.tensor_tensor(zg[:, n0:D].rearrange("p (e r) -> p e r", r=RANK),
                                      ps_w0[:, 0:HALF].rearrange("p (e r) -> p e r", r=RANK),
                                      gate[:, E0:E].unsqueeze(2).broadcast_to([P, E - E0, RANK]),
                                      ALU.mult).then_inc(zg_ok, 1)
                if first(f):
                    for k in range(2):
                        dve.wait_ge(b_h, k + 3)
                        dve.tensor_tensor(b_lo[:, k + 2, :], b_sb[:, k + 2, :], b_hi[:, k + 2, :].bitcast(F32),
                                          ALU.subtract).then_inc(b_l2, 1)

            pipeline(dve, step)

        @block.tensor
        def _(pe):
            def product(dst, hi, lo, w_hi, w_lo, cols, chunks=range(DK)):
                for k in chunks:
                    pe.matmul(dst, hi(k), w_hi[:, k, cols], start=(k == 0), stop=False)
                    pe.matmul(dst, hi(k), w_lo[:, k, cols], start=False, stop=False)
                    mm = pe.matmul(dst, lo(k), w_hi[:, k, cols], start=False, stop=(k == DK - 1))
                return mm

            def chunk(t):
                return lambda k: t[:, k, :]

            def turn(dst, src, n):
                for k in range(n):
                    mm = pe.transpose(dst[:, P * k:P * (k + 1)], src[:, P * k:P * (k + 1)], ident[:])
                return mm

            pe.wait_ge(warm_ok, 1)
            for _ in range(WARM):
                pe.matmul(ps_t0[:], warm[:, 0:P], warm[:], start=True, stop=True)

            def step(p, a, f, g):
                def scores(u):
                    b, rp = u // 2, u % 2
                    if u == 0:
                        pe.wait_ge(qT_hi_ok, nth(1, a, 1))
                        pe.wait_ge(qT_lo_ok, nth(1, a, 1))
                        pe.wait_ge(k_bd_ok, nth(2, a, 2))
                    if later(a) or u >= 2:
                        pe.wait_ge(exp_ok, nth(U, a, u - 1))
                    dst = ps_s[:, u % 2, :]
                    q_hi, q_lo = (q[:, b, 2 * rp:2 * rp + 2, :].rearrange("p r q -> p (r q)") for q in (qT_hi, qT_lo))
                    k_hi, k_lo = (k[:, b].rearrange("p h k -> p (h k)") for k in (k_bd_hi, k_bd_lo))
                    pe.matmul(dst, q_hi, k_hi, start=True, stop=False)
                    pe.matmul(dst, q_hi, k_lo, start=False, stop=False)
                    pe.matmul(dst, q_lo, k_hi, start=False, stop=True).then_inc(s_ps, 1)

                def turn_unit(u):
                    pe.wait_ge(prob_ok, nth(U, a, u + 1))
                    if later(a) or u >= 1:
                        pe.wait_ge(pT_ok, nth(U, a, u))
                    turn(ps_d, prob[:, u % 2, :], PAIRS).then_inc(pT_ps, 1)

                def values(t, b):
                    pe.wait_ge(pT_ok, nth(U, t, 2 * b + 2))
                    pe.wait_ge(v_bd_ok, nth(4, t, 4))
                    if b == 1 or later(t):
                        pe.wait_ge(oT_lo_ok, nth(2, t, b))
                    else:
                        pe.wait_ge(route_w, 2)
                    for c in range(PAIRS):
                        mm = pe.matmul(ps_o[32 * c:32 * c + 32, b, :], v_bd[:, b, c, :], pT[:, b, c, :],
                                       start=True, stop=True)
                    mm.then_inc(o_ps, 1)

                def project_q(chunks):
                    return product(ps_w0[:], chunk(xT_hi), chunk(xT_lo), wq_hi, wq_lo, slice(0, D), chunks)

                if a is not None:
                    scores(0)
                    scores(1)
                if first(p):
                    pe.wait_ge(const_ok, 1)
                    for k in range(DK):
                        pe.wait_ge(ld_wq[k], 16)
                        mm = pe.matmul(ps_w0[:], mean_w[:], wq_sb[:, k, :], start=(k == 0), stop=(k == DK - 1))
                    mm.then_inc(mean_q, 1)
                if g is not None:
                    pe.wait_ge(zg_ok, nth(2, g, 2))
                    pe.wait_ge(kT_lo_ok, T if p is None else p)
                    turn(ps_t1, zg, DK).then_inc(zT_ps, 1)
                if f is not None:
                    values(f, 1)
                if p is not None:
                    if first(p):
                        pe.wait_ge(wkv_l, 1)
                    pe.wait_ge(c_hi_ok, nth(1, p, 1))
                    pe.wait_ge(c_lo_ok, nth(1, p, 1))
                    if g is not None:
                        pe.wait_ge(zg_ok, nth(2, g, 1))
                    elif later(p):
                        pe.wait_ge(v_st_ok, nth(1, p, 0))
                    product(ps_w1[:, 0:2 * KV], chunk(cT_hi), chunk(cT_lo), wkv_hi, wkv_lo, slice(0, 2 * KV))\
                        .then_inc(kv_ps, 1)
                if first(p):
                    pe.wait_ge(ld["wr"], 16)
                    pe.wait_ge(ld["keys"], 16)
                    for k in range(DK):
                        mm = pe.matmul(ROUTE[:, E * k:E * (k + 1)], wr_sb[:, P * k:P * (k + 1)], keysT_sb[:],
                                       start=True, stop=True)
                    mm.then_inc(route_w, 1)
                if g is not None:
                    if first(g):
                        pe.wait_ge(b_l, 2)
                        pe.wait_ge(b_l2, 2)
                    pe.wait_ge(zT_hi_ok, nth(1, g, 1))
                    pe.wait_ge(zT_lo_ok, nth(1, g, 1))
                    product(ps_w0[:], chunk(zT_hi), chunk(zT_lo), b_hi, b_lo, slice(0, D)).then_inc(out_ps, 1)
                if first(a):
                    pe.wait_ge(ld["am"], 16)
                    pe.wait_ge(route_w, 2)
                    pe.wait_ge(q_rot, 2)
                    pe.wait_ge(qT_lo_ok, 1)
                    for dst, c in ((MEAN_A, slice(0, HALF)), (MEAN_B, slice(HALF, AM))):
                        for k in range(DK):
                            mm = pe.matmul(dst, mean_w[:], am_sb[:, k, c], start=(k == 0), stop=(k == DK - 1))
                    mm.then_inc(mean_am, 1)
                if a is not None:
                    scores(2)
                if p is not None:
                    pe.wait_ge(k_rot, nth(3, p, 3))
                    if first(p):
                        pe.wait_ge(const_ok, 12)
                    elif g is not None:
                        pe.wait_ge(zT_lo_ok, nth(1, g, 1))
                    else:
                        pe.wait_ge(kT_lo_ok, nth(1, p, 0))
                    pe.transpose(ps_t1[:, 0:P], k_r[:], ident[:]).then_inc(kT_ps, 1)
                if a is not None:
                    turn_unit(0)
                if f is not None:
                    if first(f):
                        pe.wait_ge(wo_h, REP)
                        pe.wait_ge(wo_l, REP)
                    pe.wait_ge(oT_hi_ok, nth(2, f, 2))
                    pe.wait_ge(oT_lo_ok, nth(2, f, 2))
                    if p is not None:
                        pe.wait_ge(v_st_ok, nth(1, p, 1))
                    else:
                        pe.wait_ge(zg_ok, nth(2, g, 1))
                    product(ps_w1[:], *(lambda k, o=o: o[:, k].rearrange("p b q -> p (b q)") for o in (oT_hi, oT_lo)),
                            wo_hi, wo_lo, slice(0, D)).then_inc(y_ps, 1)
                if a is not None:
                    scores(3)
                    turn_unit(1)
                if p is not None:
                    pe.wait_ge(x_hi_ok, nth(1, p, 1))
                    pe.wait_ge(x_lo_ok, nth(1, p, 1))
                    if first(p):
                        pe.wait_ge(wq_l0, 1)
                        project_q([0])
                        for k in range(1, DK):
                            pe.wait_ge(wq_l, k)
                            mm = project_q([k])
                        mm.then_inc(q_ps, 1)
                    else:
                        if g is not None:
                            pe.wait_ge(res_ok, nth(1, g, 1))
                        elif f is not None:
                            pe.wait_ge(q_rot, nth(2, p, 0))
                        else:
                            pe.wait_ge(am_cent, DK)
                        project_q(range(DK // 2))
                if f is not None:
                    pe.wait_ge(x2_ok, nth(1, f, 1))
                    pe.wait_ge(qT_lo_ok, T if p is None else p)
                    turn(ps_t0, x2, DK).then_inc(x2T_ps, 1)
                if p is not None and later(p):
                    project_q(range(DK // 2, DK)).then_inc(q_ps, 1)
                if a is not None:
                    turn_unit(2)
                    values(a, 0)
                    turn_unit(3)
                if f is not None:
                    if first(f):
                        pe.wait_ge(am_h, DK)
                        pe.wait_ge(am_l, DK)
                    pe.wait_ge(x2T_hi_ok, nth(1, f, 1))
                    pe.wait_ge(x2T_lo_ok, nth(1, f, 1))
                    product(ps_w1[:, 0:HALF], chunk(x2T_hi), chunk(x2T_lo), am_hi, am_lo, slice(0, HALF))\
                        .then_inc(z_ps, 1)
                if p is not None:
                    pe.wait_ge(q_r_ok, nth(1, p, 1))
                    if f is not None:
                        pe.wait_ge(x2T_lo_ok, nth(1, f, 1))
                    elif first(a):
                        pe.wait_ge(am_cent, 2 * DK)
                    turn(ps_t0, q_r, REP).then_inc(qT_ps, 1)
                if f is not None:
                    if p is not None:
                        pe.wait_ge(q_rot, nth(2, p, 2))
                    elif g is not None:
                        pe.wait_ge(res_ok, nth(1, g, 1))
                    product(ps_w0[:, 0:HALF], chunk(x2T_hi), chunk(x2T_lo), am_hi, am_lo, slice(HALF, AM))\
                        .then_inc(z_ps, 1)

            pipeline(pe, step)


def kernel(x, ctx_4096, itok_BxS2_0_2047, L0_xattn_Wq, L0_xattn_Wk, L0_xattn_Wv, L0_xattn_Wo,
           L0_ffn_A_w, L0_ffn_B_w, L0_ffn_Wq_w, L0_ffn_keys):
    import concourse.bacc as bacc
    from concourse.bass_utils import run_bass_kernel_spmd

    def rows(w):
        return w.reshape(DK, P, -1).transpose(1, 0, 2)

    def turned(a):
        return a.reshape(T, P, DK, P).transpose(0, 3, 2, 1)

    x, c = np.asarray(x), np.asarray(ctx_4096)
    wo = np.asarray(L0_xattn_Wo).reshape(KVH, REP, HD, D).transpose(0, 2, 1, 3).reshape(KV, REP, D)
    arrays = {
        "x": x.reshape(T, P, D),
        "xT": turned(x.reshape(TOKENS, D)),
        "cT": turned(c.reshape(TOKENS, D)),
        "pos": np.asarray(itok_BxS2_0_2047).reshape(T, P).T,
        "wq": rows(np.asarray(L0_xattn_Wq)),
        "wkv": rows(np.concatenate([np.asarray(L0_xattn_Wk), np.asarray(L0_xattn_Wv)], axis=1)),
        "wo": wo,
        "aT": rows(np.asarray(L0_ffn_A_w).T),
        "wr": np.asarray(L0_ffn_Wq_w),
        "keysT": np.asarray(L0_ffn_keys).T,
        "bT": rows(np.asarray(L0_ffn_B_w).T),
    }
    arrays = {n: np.ascontiguousarray(a) for n, a in arrays.items()}
    nc = bacc.Bacc("TRN2", target_bir_lowering=False, num_devices=1)
    ins = [nc.dram_tensor(n, a.shape, mybir.dt.from_np(a.dtype), kind="ExternalInput").ap()
           for n, a in arrays.items()]
    out = nc.dram_tensor("out", (T, P, D), F32, kind="ExternalOutput").ap()
    build(nc, *ins, out)
    r = run_bass_kernel_spmd(nc, [arrays], core_ids=[0])
    return r.results[0]["out"].reshape(16, BATCH, D)
```

```python
import numpy as np
import concourse.bass as bass
from concourse import mybir
from contextlib import ExitStack

F32 = mybir.dt.float32
F32R = mybir.dt.float32r
I32 = mybir.dt.int32
ALU = mybir.AluOpType
ACT = mybir.ActivationFunctionType
AX = mybir.AxisListType

P = 128
BATCH = 64
D = 512
DK = D // P
HD = 16
KVH = 8
REP = 4
PAIRS = KVH // 2
KV = KVH * HD
E = 64
RANK = 8
TOP = 16
ROUTER = 16
AM = E + D
HALF = AM // 2
E0 = (HALF - E) // RANK
TOKENS = 1024
T = TOKENS // P
U = 4
EPS = 1e-5
SCALE = float(HD) ** -0.5
GATE_SCALE = 32 / TOP
STEPS = 12
WARM = 4
TAKEN = -3.0e38
MAGIC = 1.5 * 2.0 ** 23
TWO_PI = 2 * np.pi
PI_A = float(np.round(TWO_PI * 2 ** 8) / 2 ** 8)
PI_B = float(np.round((TWO_PI - PI_A) * 2 ** 20) / 2 ** 20)
PI_C = float(np.float32(TWO_PI - PI_A - PI_B))
PI_LOW = float(np.nextafter(np.float32(np.pi), np.float32(0)))


def nth(per, t, k):
    return per * t + k


def first(t):
    return isinstance(t, int) and t == 0


def later(t):
    return not first(t)


def build(nc, x, xT, cT, pos, wq, wkv, wo, aT, router, bT, out):
    ctx = ExitStack()
    with ctx:
        def sb(name, shape, dt=F32):
            return ctx.enter_context(nc.sbuf_tensor(name, shape, dt))

        def pb(name, shape):
            return ctx.enter_context(nc.psum_tensor(name, shape, F32))

        def sem(name):
            return ctx.enter_context(nc.semaphore(name))

        x_sb = sb("x_sb", [P, T, D])
        xT_in = sb("xT_in", [P, DK, P])
        cT_in = sb("cT_in", [P, DK, P])
        wq_sb = sb("wq_sb", [P, DK, D])
        wkv_sb = sb("wkv_sb", [P, DK, 2 * KV])
        wo_sb = sb("wo_sb", [P, REP, D])
        am_sb = sb("am_sb", [P, DK, AM])
        router_sb = sb("router_sb", [ROUTER, D + E])
        pos_sb = sb("pos_sb", [P, T], I32)
        wq_hi, wq_lo = sb("wq_hi", [P, DK, D], F32R), sb("wq_lo", [P, DK, D], F32R)
        wkv_hi, wkv_lo = sb("wkv_hi", [P, DK, 2 * KV], F32R), sb("wkv_lo", [P, DK, 2 * KV], F32R)
        wo_hi, wo_lo = sb("wo_hi", [P, REP, D], F32R), sb("wo_lo", [P, REP, D], F32R)
        am_hi, am_lo = sb("am_hi", [P, DK, AM], F32R), sb("am_lo", [P, DK, AM], F32R)
        b_hi, b_lo = sb("b_hi", [P, DK, D], F32R), sb("b_lo", [P, DK, D], F32R)
        b_sb = wq_sb
        warm = sb("warm", [P, D], mybir.dt.bfloat16)
        ident = sb("ident", [P, P])
        mean_w = sb("mean_w", [P, P])
        head_mask = sb("head_mask", [P, KVH])
        freq = sb("freq", [P, HD // 2])
        preload = sb("preload", [P, 2])
        half_pi = sb("half_pi", [P, 1])
        neg_half = sb("neg_half", [P, 1])
        pos_f = sb("pos_f", [P, T])
        ang = sb("ang", [P, T, HD // 2])
        turns = sb("turns", [P, T, HD // 2])
        rem = sb("rem", [P, 3, T, HD // 2])
        abs_r = sb("abs_r", [P, T, HD // 2])
        cs = sb("cs", [P, T, 2 * HD])
        cs_q = sb("cs_q", [P, 2 * HD])
        xT_hi, xT_lo = sb("xT_hi", [P, DK, P], F32R), sb("xT_lo", [P, DK, P], F32R)
        cT_hi, cT_lo = sb("cT_hi", [P, DK, P], F32R), sb("cT_lo", [P, DK, P], F32R)
        bn1, mv1, ve1, rstd1 = sb("bn1", [P, 6]), sb("mv1", [P, 2]), sb("ve1", [P, 1]), sb("rstd1", [P, 1])
        q_a, q_b, q_r = sb("q_a", [P, D]), sb("q_b", [P, D]), sb("q_r", [P, D])
        k_a, k_b, k_r = sb("k_a", [P, KV]), sb("k_b", [P, KV]), sb("k_r", [P, KV])
        v_st = sb("v_st", [P, KV])
        kT_hi, kT_lo = sb("kT_hi", [P, P], F32R), sb("kT_lo", [P, P], F32R)
        qT_hi, qT_lo = sb("qT_hi", [P, 2, REP, BATCH], F32R), sb("qT_lo", [P, 2, REP, BATCH], F32R)
        k_bd_hi = sb("k_bd_hi", [P, 2, KVH, BATCH], F32R)
        k_bd_lo = sb("k_bd_lo", [P, 2, KVH, BATCH], F32R)
        v_bd = sb("v_bd", [P, 2, PAIRS, 2 * HD])
        neg_top = sb("neg_top", [P, U, KVH])
        e_un = sb("e_un", [P, 2, D])
        sums = sb("sums", [P, U, KVH])
        inv = sb("inv", [P, U, KVH])
        prob = sb("prob", [P, 2, D])
        pT = sb("pT", [P, 2, PAIRS, REP * BATCH])
        oT_hi = sb("oT_hi", [P, REP, 2, BATCH], F32R)
        oT_lo = sb("oT_lo", [P, REP, 2, BATCH], F32R)
        bn2, mv2, ve2, rstd2 = sb("bn2", [P, 6]), sb("mv2", [P, 2]), sb("ve2", [P, 1]), sb("rstd2", [P, 1])
        x2 = sb("x2", [P, D])
        x2_end = sb("x2_end", [P, 2, D])
        x2T_hi, x2T_lo = sb("x2T_hi", [P, DK, P], F32R), sb("x2T_lo", [P, DK, P], F32R)
        s_sb, s_a, s_b = sb("s_sb", [P, E]), sb("s_a", [P, E]), sb("s_b", [P, E])
        top_a, top_b = sb("top_a", [P, 8]), sb("top_b", [P, 8])
        neg_max, e_sum, e_inv, g_scale = (sb(n, [P, 1]) for n in ("neg_max", "e_sum", "e_inv", "g_scale"))
        e_sb, e_top, gate = sb("e_sb", [P, E]), sb("e_top", [P, E]), sb("gate", [P, E])
        zg = sb("zg", [P, D])
        zT_hi, zT_lo = sb("zT_hi", [P, DK, P], F32R), sb("zT_lo", [P, DK, P], F32R)
        res = sb("res", [P, D])

        ps_s = pb("ps_s", [P, 2, D])
        ps_d = pb("ps_d", [P, D])
        ps_o = pb("ps_o", [P, 2, REP * BATCH])
        ps_w0, ps_w1 = pb("ps_w0", [P, D]), pb("ps_w1", [P, D])
        ps_t0, ps_t1 = pb("ps_t0", [P, D]), pb("ps_t1", [P, D])
        MEAN_A, MEAN_B = ps_w1[:, 0:HALF], ps_d[:, 0:HALF]
        ROUTE = ps_o[:].rearrange("p b n -> p (b n)")[:, 0:DK * E]

        def is_last(t):
            return isinstance(t, int) and t == T - 1

        def x2_of(t):
            return x2_end[:, t - (T - 2), :] if isinstance(t, int) and t >= T - 2 else x2[:]

        def y_bank(t):
            return ps_s[:, 0, :] if is_last(t) else ps_w1[:]

        def z_bank(t, half):
            if is_last(t):
                return (ps_d[:], ps_o[:].rearrange("p b n -> p (b n)"))[half]
            return (ps_w1[:], ps_w0[:])[half]

        def out_bank(t):
            return ps_w1[:] if is_last(t) else ps_w0[:]

        ld = {n: sem("ld_" + n) for n in ("c", "x", "xnat0", "xnat", "pos", "wkv", "wo", "am",
                                           "router", "b")}
        ld_wq = [sem(f"ld_wq{k}") for k in range(DK)]
        warm_ok = sem("warm_ok")
        const_ok = sem("const_ok")
        mask_step = sem("mask_step")
        rope_step = sem("rope_step")
        cs_ok = sem("cs_ok")
        mean_q = sem("mean_q")
        wq_cent = sem("wq_cent")
        wq_h = sem("wq_h")
        wq_l0, wq_l = sem("wq_l0"), sem("wq_l")
        wkv_h, wkv_l = sem("wkv_h"), sem("wkv_l")
        wo_h, wo_l = sem("wo_h"), sem("wo_l")
        route_w = sem("route_w")
        mean_am = sem("mean_am")
        am_cent = sem("am_cent")
        am_h, am_l = sem("am_h"), sem("am_l")
        b_h, b_l, b_l2 = sem("b_h"), sem("b_l"), sem("b_l2")
        c_hi_ok, c_lo_ok, x_hi_ok, x_lo_ok = sem("c_hi_ok"), sem("c_lo_ok"), sem("x_hi_ok"), sem("x_lo_ok")
        stat1 = sem("stat1")
        rstd1_ok = sem("rstd1_ok")
        cs_q_ok = sem("cs_q_ok")
        kv_ps, q_ps = sem("kv_ps"), sem("q_ps")
        k_rot = sem("k_rot")
        v_st_ok = sem("v_st_ok")
        q_rot = sem("q_rot")
        q_r_ok = sem("q_r_ok")
        kT_ps, qT_ps = sem("kT_ps"), sem("qT_ps")
        kT_hi_ok, kT_lo_ok = sem("kT_hi_ok"), sem("kT_lo_ok")
        qT_hi_ok, qT_lo_ok = sem("qT_hi_ok"), sem("qT_lo_ok")
        k_bd_ok = sem("k_bd_ok")
        v_bd_ok = sem("v_bd_ok")
        s_ps = sem("s_ps")
        max_ok = sem("max_ok")
        exp_ok = sem("exp_ok")
        diff_ok = sem("diff_ok")
        sum_ok = sem("sum_ok")
        inv_ok = sem("inv_ok")
        prob_ok = sem("prob_ok")
        pT_ps = sem("pT_ps")
        pT_ok = sem("pT_ok")
        o_ps = sem("o_ps")
        oT_hi_ok, oT_lo_ok = sem("oT_hi_ok"), sem("oT_lo_ok")
        y_ps = sem("y_ps")
        x2_ok = sem("x2_ok")
        stat2 = sem("stat2")
        rstd2_ok = sem("rstd2_ok")
        x2T_ps, x2T_hi_ok, x2T_lo_ok = sem("x2T_ps"), sem("x2T_hi_ok"), sem("x2T_lo_ok")
        z_ps = sem("z_ps")
        s_ok = sem("s_ok")
        top_step = sem("top_step")
        e_ok = sem("e_ok")
        zg_ok = sem("zg_ok")
        zT_ps, zT_hi_ok, zT_lo_ok = sem("zT_ps"), sem("zT_hi_ok"), sem("zT_lo_ok")
        out_ps = sem("out_ps")
        res_ok = sem("res_ok")
        stored = sem("stored")

        block = ctx.enter_context(nc.Block())

        def pipeline(eng, step, finish):
            def tiles(i):
                return [t if t >= 0 else None for t in (i + 1, i, i - 1, i - 2)]
            for i in (-1, 0, 1, 2):
                step(*tiles(i))
            with eng.Fori(3, T - 1) as i:
                step(i + 1, i, i - 1, i - 2)
            finish(*tiles(T - 1))

        @block.sync
        def _(sp):
            def load(dst, src, name):
                sp.dma_start(dst, src).then_inc(ld[name], 16)

            for k in range(DK):
                sp.dma_start(wq_sb[:, k, :], wq[:, k, :]).then_inc(ld_wq[k], 16)
            load(xT_in[:], xT[0], "x")
            load(router_sb[:], router, "router")
            load(x_sb[:, 0, :], x[0], "xnat0")
            load(am_sb[:, :, E:AM], aT, "am")
            load(wo_sb[:], wo, "wo")
            load(x_sb[:, 1:T, :], x[1:T].rearrange("t p d -> p t d"), "xnat")

            def load_tile(t):
                sp.wait_ge(c_hi_ok, t)
                sp.wait_ge(c_lo_ok, t)
                load(cT_in[:], cT[t], "c")
                sp.wait_ge(x_hi_ok, t)
                sp.wait_ge(x_lo_ok, t)
                load(xT_in[:], xT[t], "x")

            def store_tile(t):
                sp.wait_ge(res_ok, t + 1)
                sp.dma_start(out[t], res[:]).then_inc(stored, 16)

            load_tile(1)
            sp.wait_ge(wq_h, DK)
            sp.wait_ge(wq_l0, 1)
            sp.wait_ge(wq_l, DK - 1)
            load(b_sb[:], bT, "b")
            with sp.Fori(2, 4) as t:
                load_tile(t)
            with sp.Fori(4, T) as t:
                load_tile(t)
                store_tile(t - 4)
            with sp.Fori(T - 4, T) as t:
                store_tile(t)
            sp.wait_ge(stored, 16 * T)

        @block.gpsimd
        def _(pool):
            pool.memset(mean_w[:], 1.0 / D).then_inc(const_ok, 1)
            for j in range(HD // 2):
                f = np.float32(1.0) / np.float32(10000.0) ** np.float32(2 * j / HD)
                pool.memset(freq[:, j:j + 1], float(f)).then_inc(const_ok, 1)
            pool.memset(half_pi[:], float(np.pi / 2)).then_inc(const_ok, 1)
            pool.memset(neg_half[:], -0.5).then_inc(const_ok, 1)
            pool.memset(v_bd[:], 0.0).then_inc(mask_step, 1)
            pool.memset(head_mask[:], SCALE).then_inc(mask_step, 1)
            pool.memset(ident[:], 0.0).then_inc(mask_step, 1)
            pool.wait_ge(mask_step, 3)
            pool.affine_select(out=ident[:], in_=ident[:], compare_op=ALU.not_equal, fill=1.0, base=0,
                               pattern=[[-1, P]], channel_multiplier=1).then_inc(const_ok, 1)
            pool.affine_select(out=head_mask[:], in_=head_mask[:], compare_op=ALU.is_ge, fill=0.0, base=0,
                               pattern=[[-HD, KVH]], channel_multiplier=1).then_inc(mask_step, 1)
            pool.wait_ge(mask_step, 4)
            pool.affine_select(out=head_mask[:], in_=head_mask[:], compare_op=ALU.is_ge, fill=0.0, base=HD - 1,
                               pattern=[[HD, KVH]], channel_multiplier=-1).then_inc(const_ok, 1)

            def split_lo(lo, raw, hi, high, low, k):
                pool.wait_ge(high, k + 1)
                pool.tensor_tensor(lo[:, k, :], raw[:, k, :], hi[:, k, :].bitcast(F32),
                                   ALU.subtract).then_inc(low, 1)

            def normalise(a, u):
                pool.wait_ge(inv_ok, nth(U, a, u + 1))
                if later(a) or u >= 2:
                    pool.wait_ge(pT_ps, nth(U, a, u - 1))
                pool.tensor_tensor(prob[:, u % 2, :].rearrange("p (h k) -> p h k", h=KVH),
                                   e_un[:, u % 2, :].rearrange("p (h k) -> p h k", h=KVH),
                                   inv[:, u, :].unsqueeze(2).broadcast_to([P, KVH, BATCH]),
                                   ALU.mult).then_inc(prob_ok, 1)

            def c_low(p):
                pool.wait_ge(c_hi_ok, nth(1, p, 1))
                if later(p):
                    pool.wait_ge(kv_ps, nth(1, p, 0))
                pool.tensor_tensor(cT_lo[:], cT_in[:], cT_hi[:].bitcast(F32), ALU.subtract).then_inc(c_lo_ok, 1)

            def x_low(p):
                pool.wait_ge(x_hi_ok, nth(1, p, 1))
                if later(p):
                    pool.wait_ge(q_ps, nth(1, p, 0))
                pool.tensor_tensor(xT_lo[:], xT_in[:], xT_hi[:].bitcast(F32), ALU.subtract).then_inc(x_lo_ok, 1)

            def deviation1(p):
                pool.wait_ge(stat1, nth(3, p, 3))
                if later(p):
                    pool.wait_ge(cs_q_ok, nth(1, p, 0))
                pool.tensor_tensor(rstd1[:], ve1[:], neg_half[:], ALU.pow).then_inc(rstd1_ok, 1)

            def deviation2(f):
                pool.wait_ge(stat2, nth(3, f, 3))
                if later(f):
                    pool.wait_ge(top_step, nth(STEPS, f, 0))
                    pool.wait_ge(e_ok, nth(1, f, 0))
                pool.tensor_tensor(rstd2[:], ve2[:], neg_half[:], ALU.pow).then_inc(rstd2_ok, 1)

            def k_blocks(p, n):
                bd, kT, ok = ((k_bd_hi, kT_hi, kT_hi_ok), (k_bd_lo, kT_lo, kT_lo_ok))[n]
                pool.wait_ge(ok, nth(1, p, 1))
                if later(p):
                    pool.wait_ge(s_ps, nth(U, p, 0))
                pool.tensor_tensor(
                    bd[:],
                    kT[:].bitcast(F32).rearrange("p (b q) -> p b q", b=2).unsqueeze(2)
                    .broadcast_to([P, 2, KVH, BATCH]),
                    head_mask[:].unsqueeze(1).unsqueeze(3).broadcast_to([P, 2, KVH, BATCH]),
                    ALU.mult).then_inc(k_bd_ok, 1)

            def step(p, a, f, g):
                c_low(p)
                if first(p):
                    x_low(p)
                    split_lo(wq_lo, wq_sb, wq_hi, wq_h, wq_l0, 0)
                    k_blocks(p, 0)
                    deviation1(p)
                    k_blocks(p, 1)
                    split_lo(wo_lo, wo_sb, wo_hi, wo_h, wo_l, 0)
                    return
                if g is None:
                    x_low(p)
                if first(f):
                    split_lo(wo_lo, wo_sb, wo_hi, wo_h, wo_l, 2)
                    split_lo(wo_lo, wo_sb, wo_hi, wo_h, wo_l, 3)
                if first(a):
                    deviation1(p)
                normalise(a, 0)
                if first(f):
                    split_lo(b_lo, b_sb, b_hi, b_h, b_l, 0)
                    split_lo(b_lo, b_sb, b_hi, b_h, b_l, 1)
                normalise(a, 1)
                if later(a):
                    if g is not None:
                        x_low(p)
                    deviation1(p)
                    normalise(a, 2)
                    k_blocks(p, 0)
                else:
                    k_blocks(p, 0)
                    normalise(a, 2)
                normalise(a, 3)
                if f is not None:
                    deviation2(f)
                k_blocks(p, 1)
                if first(a):
                    split_lo(wo_lo, wo_sb, wo_hi, wo_h, wo_l, 1)

            def finish(p, a, f, g):
                for u in range(U):
                    normalise(a, u)
                deviation2(f)
                deviation2(a)

            pipeline(pool, step, finish)

        @block.scalar
        def _(act):
            for dst, src, name in ((pos_sb[:], pos, "pos"), (wkv_sb[:], wkv, "wkv"), (cT_in[:], cT[0], "c")):
                act.dma_start(dst, src).then_inc(ld[name], 16)
            act.wait_ge(const_ok, 10)
            act.activation(preload[:, 0:1], half_pi[:], ACT.Sin)
            act.wait_ge(ld["wkv"], 16)
            act.activation(wkv_hi[:], wkv_sb[:], ACT.Copy).then_inc(wkv_h, 1)
            act.wait_ge(ld["c"], 16)
            act.activation(cT_hi[:], cT_in[:], ACT.Copy).then_inc(c_hi_ok, 1)
            act.wait_ge(rope_step, 9)
            act.activation(cs[:, :, 24:32], rem[:, 2], ACT.Sin).then_inc(cs_ok, 1)
            act.activation(cs[:, :, 16:24], rem[:, 2], ACT.Sin, scale=-1.0).then_inc(cs_ok, 1)
            for c in range(2):
                act.activation(cs[:, :, 8 * c:8 * c + 8], abs_r[:], ACT.Sin, scale=-1.0,
                               bias=half_pi[:]).then_inc(cs_ok, 1)

            def exps(a, u, heads=range(KVH)):
                act.wait_ge(max_ok, nth(U, a, u + 1))
                if later(a) or u >= 2:
                    act.wait_ge(prob_ok, nth(U, a, u - 1))
                for h in heads:
                    c = slice(BATCH * h, BATCH * (h + 1))
                    last = act.activation(e_un[:, u % 2, c], ps_s[:, u % 2, c], ACT.Exp,
                                          bias=neg_top[:, u, h:h + 1], accum_out=sums[:, u, h:h + 1])
                if h == KVH - 1:
                    last.then_inc(exp_ok, 1)

            def exps_shifted(a, u, n):
                act.wait_ge(diff_ok, n)
                act.activation(e_un[:, u % 2, :], e_un[:, u % 2, :], ACT.Exp).then_inc(exp_ok, 1)

            def turned(a, u):
                act.wait_ge(pT_ps, nth(U, a, u + 1))
                b, rp = u // 2, u % 2
                if later(a):
                    act.wait_ge(o_ps, nth(2, a, b - 1))
                act.activation(pT[:, b, :, P * rp:P * (rp + 1)],
                               ps_d[:].rearrange("p (g q) -> p g q", g=PAIRS), ACT.Copy).then_inc(pT_ok, 1)

            def o_high(a, b):
                act.wait_ge(o_ps, nth(2, a, b + 1))
                if later(a):
                    act.wait_ge(y_ps, nth(1, a, 0))
                act.activation(oT_hi[:, :, b, :], ps_o[:, b, :].rearrange("p (r q) -> p r q", r=REP),
                               ACT.Copy).then_inc(oT_hi_ok, 1)

            def c_high(p):
                act.wait_ge(ld["c"], nth(16, p, 16))
                if later(p):
                    act.wait_ge(kv_ps, nth(1, p, 0))
                    act.wait_ge(c_lo_ok, nth(1, p, 0))
                act.activation(cT_hi[:], cT_in[:], ACT.Copy).then_inc(c_hi_ok, 1)

            def x_high(p):
                act.wait_ge(ld["x"], nth(16, p, 16))
                if later(p):
                    act.wait_ge(q_ps, nth(1, p, 0))
                    act.wait_ge(x_lo_ok, nth(1, p, 0))
                act.activation(xT_hi[:], xT_in[:], ACT.Copy).then_inc(x_hi_ok, 1)

            def value_blocks(a):
                act.wait_ge(v_st_ok, nth(1, a, 1))
                if later(a):
                    act.wait_ge(o_ps, nth(2, a, 0))
                else:
                    act.wait_ge(mask_step, 3)
                for b in range(2):
                    for h in range(2):
                        act.activation(
                            v_bd[BATCH * h:BATCH * (h + 1), b, :, HD * h:HD * (h + 1)],
                            v_st[BATCH * b:BATCH * (b + 1), :]
                            .rearrange("p (g h d) -> p g h d", g=PAIRS, h=2)[:, :, h, :],
                            ACT.Copy).then_inc(v_bd_ok, 1)

            def values_out(p):
                act.wait_ge(k_rot, nth(3, p, 2))
                act.wait_ge(kv_ps, nth(1, p, 1))
                if later(p):
                    act.wait_ge(v_bd_ok, nth(4, p, 0))
                act.activation(v_st[:], ps_w1[:, KV:2 * KV], ACT.Copy).then_inc(v_st_ok, 1)

            def k_high(p):
                act.wait_ge(kT_ps, nth(1, p, 1))
                if later(p):
                    act.wait_ge(k_bd_ok, nth(2, p, 0))
                act.activation(kT_hi[:], ps_t1[:, 0:P], ACT.Copy).then_inc(kT_hi_ok, 1)

            def q_high(p):
                act.wait_ge(qT_ps, nth(1, p, 1))
                if later(p):
                    act.wait_ge(s_ps, nth(U, p, 0))
                act.activation(qT_hi[:].rearrange("p b r q -> p r b q"),
                               ps_t0[:].rearrange("p (r b q) -> p r b q", r=REP, b=2),
                               ACT.Copy).then_inc(qT_hi_ok, 1)

            def x2_high(f):
                act.wait_ge(x2T_ps, nth(1, f, 1))
                if later(f):
                    act.wait_ge(z_ps, nth(2, f, 0))
                act.activation(x2T_hi[:], ps_t0[:].rearrange("p (k q) -> p k q", k=DK), ACT.Copy)\
                   .then_inc(x2T_hi_ok, 1)

            def expert_scores(f):
                act.wait_ge(z_ps, nth(2, f, 1))
                if later(f):
                    act.wait_ge(top_step, nth(STEPS, f, 0))
                act.activation(s_sb[:], z_bank(f, 0)[:, 0:E], ACT.Copy).then_inc(s_ok, 1)

            def expert_exps(f):
                act.wait_ge(s_ok, nth(1, f, 1))
                act.wait_ge(rstd2_ok, nth(1, f, 1))
                act.wait_ge(top_step, nth(STEPS, f, 3))
                act.activation(e_sb[:], s_sb[:], ACT.Exp, scale=rstd2[:], bias=neg_max[:]).then_inc(e_ok, 1)

            def z_high(g):
                act.wait_ge(zT_ps, nth(1, g, 1))
                for h in (slice(0, 2), slice(2, DK)):
                    act.activation(zT_hi[:, h, :], ps_t1[:].rearrange("p (k q) -> p k q", k=DK)[:, h, :],
                                   ACT.Copy).then_inc(zT_hi_ok, 1)

            def step(p, a, f, g):
                if first(p):
                    x_high(p)
                    for k in range(DK):
                        act.wait_ge(wq_cent, k + 1)
                        act.activation(wq_hi[:, k, :], wq_sb[:, k, :], ACT.Copy).then_inc(wq_h, 1)
                    values_out(p)
                    k_high(p)
                    act.wait_ge(route_w, 1)
                    act.activation(am_sb[:, :, 0:E], ROUTE.rearrange("p (k e) -> p k e", k=DK),
                                   ACT.Copy).then_inc(route_w, 1)
                    act.activation(preload[:, 1:2], half_pi[:], ACT.Exp)
                    act.wait_ge(ld["wo"], 16)
                    for k in range(REP):
                        act.activation(wo_hi[:, k, :], wo_sb[:, k, :], ACT.Copy).then_inc(wo_h, 1)
                    q_high(p)
                    return
                c_high(p)
                if g is None:
                    x_high(p)
                if f is not None:
                    o_high(f, 1)
                if g is not None:
                    z_high(g)
                exps(a, 0)
                if first(a):
                    exps(a, 1)
                    k_high(p)
                    exps(a, 2)
                    turned(a, 0)
                    exps(a, 3)
                    turned(a, 1)
                    value_blocks(a)
                    values_out(p)
                    turned(a, 2)
                    q_high(p)
                    o_high(a, 0)
                    turned(a, 3)
                    return
                value_blocks(a)
                values_out(p)
                exps(a, 1)
                k_high(p)
                turned(a, 0)
                if g is not None:
                    x_high(p)
                exps(a, 2)
                turned(a, 1)
                exps(a, 3, range(KVH // 2))
                x2_high(f)
                exps(a, 3, range(KVH // 2, KVH))
                turned(a, 2)
                o_high(a, 0)
                expert_scores(f)
                turned(a, 3)
                q_high(p)
                expert_exps(f)

            def finish(p, a, f, g):
                o_high(f, 1)
                exps(a, 0)
                exps_shifted(a, 1, 1)
                z_high(g)
                turned(a, 0)
                x2_high(f)
                exps(a, 2)
                turned(a, 1)
                exps_shifted(a, 3, 2)
                value_blocks(a)
                expert_scores(f)
                turned(a, 2)
                o_high(a, 0)
                expert_exps(f)
                turned(a, 3)
                o_high(a, 1)
                z_high(f)
                x2_high(a)
                expert_scores(a)
                expert_exps(a)
                z_high(a)

            pipeline(act, step, finish)

        @block.vector
        def _(dve):
            dve.memset(warm[:], 0.0).then_inc(warm_ok, 1)
            dve.wait_ge(ld["pos"], 16)
            dve.tensor_copy(pos_f[:], pos_sb[:]).then_inc(rope_step, 1)
            dve.wait_ge(rope_step, 1)
            dve.wait_ge(const_ok, 9)
            J = HD // 2
            dve.tensor_tensor(ang[:], pos_f[:].unsqueeze(2).broadcast_to([P, T, J]),
                              freq[:].unsqueeze(1).broadcast_to([P, T, J]), ALU.mult).then_inc(rope_step, 1)
            dve.wait_ge(rope_step, 2)
            dve.tensor_scalar(turns[:], ang[:], float(1 / TWO_PI), MAGIC, ALU.mult, ALU.add).then_inc(rope_step, 1)
            dve.wait_ge(rope_step, 3)
            dve.tensor_scalar(turns[:], turns[:], MAGIC, None, ALU.subtract).then_inc(rope_step, 1)
            dve.wait_ge(rope_step, 4)
            for n, (part, src) in enumerate(((PI_A, ang[:]), (PI_B, rem[:, 0]), (PI_C, rem[:, 1]))):
                dve.scalar_tensor_tensor(rem[:, n], turns[:], -part, src, ALU.mult, ALU.add)\
                   .then_inc(rope_step, 1)
                dve.wait_ge(rope_step, 5 + n)
            dve.tensor_scalar(rem[:, 2], rem[:, 2], PI_LOW, -PI_LOW, ALU.min, ALU.max).then_inc(rope_step, 1)
            dve.wait_ge(rope_step, 8)
            dve.scalar_tensor_tensor(abs_r[:], rem[:, 2], -1.0, rem[:, 2], ALU.mult, ALU.max)\
               .then_inc(rope_step, 1)
            dve.wait_ge(wkv_h, 1)
            dve.tensor_tensor(wkv_lo[:], wkv_sb[:], wkv_hi[:].bitcast(F32), ALU.subtract).then_inc(wkv_l, 1)

            def split_hi(raw, hi, high, k):
                dve.tensor_copy(hi[:, k, :], raw[:, k, :]).then_inc(high, 1)

            def split_lo(lo, raw, hi, high, low, k):
                dve.wait_ge(high, k + 1)
                dve.tensor_tensor(lo[:, k, :], raw[:, k, :], hi[:, k, :].bitcast(F32), ALU.subtract)\
                   .then_inc(low, 1)

            def split_am(k):
                split_hi(am_sb, am_hi, am_h, k)
                split_lo(am_lo, am_sb, am_hi, am_h, am_l, k)

            def am_centre(cols, mean, n):
                dve.wait_ge(mean_am, n)
                for k in range(DK):
                    dve.tensor_tensor(am_sb[:, k, cols], am_sb[:, k, cols], mean, ALU.subtract)\
                       .then_inc(am_cent, 1)

            def top(a, u):
                dve.wait_ge(s_ps, nth(U, a, u + 1))
                dve.tensor_reduce(neg_top[:, u, :], ps_s[:, u % 2, :].rearrange("p (h k) -> p h k", h=KVH),
                                  AX.X, ALU.max, negate=True).then_inc(max_ok, 1)

            def invert(a, u):
                dve.wait_ge(exp_ok, nth(U, a, u + 1))
                dve.reciprocal(inv[:, u, :], sums[:, u, :]).then_inc(inv_ok, 1)

            def shift(a, u):
                dve.wait_ge(max_ok, nth(U, a, u + 1))
                dve.wait_ge(prob_ok, nth(U, a, u - 1))
                dve.tensor_tensor(e_un[:, u % 2, :].rearrange("p (h k) -> p h k", h=KVH),
                                  ps_s[:, u % 2, :].rearrange("p (h k) -> p h k", h=KVH),
                                  neg_top[:, u, :].unsqueeze(2).broadcast_to([P, KVH, BATCH]),
                                  ALU.add).then_inc(diff_ok, 1)

            def sum_up(a, u, n):
                dve.wait_ge(exp_ok, nth(U, a, u + 1))
                dve.reduce_sum(sums[:, u, :], e_un[:, u % 2, :].rearrange("p (h k) -> p h k", h=KVH),
                               AX.X).then_inc(sum_ok, 1)
                dve.wait_ge(sum_ok, n)

            def o_low(a, b):
                dve.wait_ge(oT_hi_ok, nth(2, a, b + 1))
                dve.tensor_tensor(oT_lo[:, :, b, :], ps_o[:, b, :].rearrange("p (r q) -> p r q", r=REP),
                                  oT_hi[:, :, b, :].bitcast(F32), ALU.subtract).then_inc(oT_lo_ok, 1)

            def table(t, at, n):
                return t[:, at:at + HD].rearrange("p (s j) -> p s j", s=2).unsqueeze(1)\
                    .broadcast_to([P, n, 2, J])

            def rotate_k(p):
                dve.wait_ge(kv_ps, nth(1, p, 1))
                k_ps = ps_w1[:, 0:KV].rearrange("p (h s j) -> p h s j", h=KVH, s=2)
                dve.tensor_tensor(k_a[:].rearrange("p (h s j) -> p h s j", h=KVH, s=2), k_ps,
                                  table(cs[:, p, :], 0, KVH), ALU.mult).then_inc(k_rot, 1)
                dve.tensor_tensor(k_b[:].rearrange("p (h s j) -> p h s j", h=KVH, s=2), k_ps[:, :, ::-1, :],
                                  table(cs[:, p, :], HD, KVH), ALU.mult).then_inc(k_rot, 1)
                dve.wait_ge(k_rot, nth(3, p, 2))
                if later(p):
                    dve.wait_ge(kT_ps, nth(1, p, 0))
                dve.tensor_tensor(k_r[:], k_a[:], k_b[:], ALU.add).then_inc(k_rot, 1)

            def k_low(p):
                dve.wait_ge(kT_hi_ok, nth(1, p, 1))
                if later(p):
                    dve.wait_ge(k_bd_ok, nth(2, p, 0))
                dve.tensor_tensor(kT_lo[:], ps_t1[:, 0:P], kT_hi[:].bitcast(F32), ALU.subtract)\
                   .then_inc(kT_lo_ok, 1)

            def statistics1(p):
                dve.wait_ge(ld["xnat0" if first(p) else "xnat"], 16)
                dve.bn_stats(bn1[:], x_sb[:, p, :]).then_inc(stat1, 1)

            def variance1(p):
                dve.bn_aggr(mv1[:], bn1[:]).then_inc(stat1, 1)
                dve.wait_ge(stat1, nth(3, p, 2))
                if later(p):
                    dve.wait_ge(rstd1_ok, nth(1, p, 0))
                dve.tensor_scalar_add(ve1[:], mv1[:, 1:2], EPS).then_inc(stat1, 1)

            def q_table(p):
                dve.wait_ge(rstd1_ok, nth(1, p, 1))
                if later(p):
                    dve.wait_ge(q_rot, nth(2, p, 0))
                dve.tensor_scalar_mul(cs_q[:], cs[:, p, :], rstd1[:]).then_inc(cs_q_ok, 1)

            def rotate_q(p, meanwhile=lambda: None):
                dve.wait_ge(q_ps, nth(1, p, 1))
                dve.wait_ge(cs_q_ok, nth(1, p, 1))
                if later(p):
                    dve.wait_ge(q_r_ok, nth(1, p, 0))
                H = REP * KVH
                w = ps_w0[:].rearrange("p (h s j) -> p h s j", h=H, s=2)
                dve.tensor_tensor(q_a[:].rearrange("p (h s j) -> p h s j", h=H, s=2), w,
                                  table(cs_q, 0, H), ALU.mult).then_inc(q_rot, 1)
                meanwhile()
                dve.tensor_tensor(q_b[:].rearrange("p (h s j) -> p h s j", h=H, s=2), w[:, :, ::-1, :],
                                  table(cs_q, HD, H), ALU.mult).then_inc(q_rot, 1)
                dve.wait_ge(q_rot, nth(2, p, 2))
                if later(p):
                    dve.wait_ge(qT_ps, nth(1, p, 0))
                dve.tensor_tensor(q_r[:].rearrange("p (r k d) -> p k r d", r=REP, k=KVH),
                                  q_a[:].rearrange("p (k r d) -> p k r d", r=REP, k=KVH),
                                  q_b[:].rearrange("p (k r d) -> p k r d", r=REP, k=KVH),
                                  ALU.add).then_inc(q_r_ok, 1)

            def q_low(p, b):
                dve.wait_ge(qT_hi_ok, nth(1, p, 1))
                dve.tensor_tensor(qT_lo[:, b], ps_t0[:].rearrange("p (r b q) -> p b r q", r=REP, b=2)[:, b],
                                  qT_hi[:, b].bitcast(F32), ALU.subtract).then_inc(qT_lo_ok, 1)

            def residual(f):
                dve.wait_ge(y_ps, nth(1, f, 1))
                if later(f) and not (isinstance(f, int) and f >= T - 2):
                    dve.wait_ge(x2T_ps, nth(1, f, 0))
                    dve.wait_ge(res_ok, nth(1, f, 0))
                dve.tensor_tensor(x2_of(f), y_bank(f), x_sb[:, f, :], ALU.add).then_inc(x2_ok, 1)

            def statistics2(f):
                dve.wait_ge(x2_ok, nth(1, f, 1))
                dve.bn_stats(bn2[:], x2_of(f)).then_inc(stat2, 1)
                dve.wait_ge(stat2, nth(3, f, 1))

            def variance2(f):
                dve.bn_aggr(mv2[:], bn2[:]).then_inc(stat2, 1)
                dve.wait_ge(stat2, nth(3, f, 2))
                if later(f):
                    dve.wait_ge(rstd2_ok, nth(1, f, 0))
                dve.tensor_scalar_add(ve2[:], mv2[:, 1:2], EPS).then_inc(stat2, 1)

            def x2_low(f):
                dve.wait_ge(x2T_hi_ok, nth(1, f, 1))
                dve.tensor_tensor(x2T_lo[:], ps_t0[:].rearrange("p (k q) -> p k q", k=DK),
                                  x2T_hi[:].bitcast(F32), ALU.subtract).then_inc(x2T_lo_ok, 1)

            def route(f, meanwhile):
                dve.wait_ge(s_ok, nth(1, f, 1))
                dve.memset(e_top[:, 0:1], 0.0).then_inc(top_step, 1)
                dve.max(top_a[:], s_sb[:]).then_inc(top_step, 1)
                dve.wait_ge(rstd2_ok, nth(1, f, 1))
                dve.wait_ge(top_step, nth(STEPS, f, 2))
                dve.tensor_scalar(neg_max[:], top_a[:, 0:1], rstd2[:], -1.0, ALU.mult, ALU.mult)\
                   .then_inc(top_step, 1)
                dve.match_replace(s_a[:], top_a[:], s_sb[:], TAKEN).then_inc(top_step, 1)
                dve.wait_ge(top_step, nth(STEPS, f, 4))
                dve.memset(e_top[:, 1:2], 0.0).then_inc(top_step, 1)
                dve.max(top_b[:], s_a[:]).then_inc(top_step, 1)
                meanwhile()
                dve.wait_ge(top_step, nth(STEPS, f, 6))
                dve.memset(e_top[:, 2:3], 0.0).then_inc(top_step, 1)
                dve.match_replace(s_b[:], top_b[:], s_a[:], TAKEN).then_inc(top_step, 1)
                dve.wait_ge(top_step, nth(STEPS, f, 8))
                dve.wait_ge(e_ok, nth(1, f, 1))
                dve.scalar_tensor_tensor(e_top[:], s_b[:], TAKEN, e_sb[:], ALU.is_equal, ALU.mult,
                                         accum_out=e_sum[:]).then_inc(top_step, 1)
                dve.wait_ge(top_step, nth(STEPS, f, 9))
                dve.reciprocal(e_inv[:], e_sum[:]).then_inc(top_step, 1)
                dve.wait_ge(top_step, nth(STEPS, f, 10))
                dve.tensor_scalar(g_scale[:], e_inv[:], rstd2[:], GATE_SCALE, ALU.mult, ALU.mult)\
                   .then_inc(top_step, 1)
                dve.wait_ge(top_step, nth(STEPS, f, 11))
                dve.tensor_scalar_mul(gate[:], e_top[:], g_scale[:]).then_inc(top_step, 1)

            def gated(f):
                dve.wait_ge(top_step, nth(STEPS, f, 12))
                if later(f):
                    dve.wait_ge(zT_ps, nth(1, f, 0))
                n0 = E0 * RANK
                dve.tensor_tensor(zg[:, 0:n0].rearrange("p (e r) -> p e r", r=RANK),
                                  z_bank(f, 0)[:, E:HALF].rearrange("p (e r) -> p e r", r=RANK),
                                  gate[:, 0:E0].unsqueeze(2).broadcast_to([P, E0, RANK]),
                                  ALU.mult).then_inc(zg_ok, 1)
                dve.wait_ge(z_ps, nth(2, f, 2))
                dve.tensor_tensor(zg[:, n0:D].rearrange("p (e r) -> p e r", r=RANK),
                                  z_bank(f, 1)[:, 0:HALF].rearrange("p (e r) -> p e r", r=RANK),
                                  gate[:, E0:E].unsqueeze(2).broadcast_to([P, E - E0, RANK]),
                                  ALU.mult).then_inc(zg_ok, 1)

            def z_low(g):
                dve.wait_ge(zT_hi_ok, nth(2, g, 2))
                for h in (slice(0, 2), slice(2, DK)):
                    dve.tensor_tensor(zT_lo[:, h, :], ps_t1[:].rearrange("p (k q) -> p k q", k=DK)[:, h, :],
                                      zT_hi[:, h, :].bitcast(F32), ALU.subtract).then_inc(zT_lo_ok, 1)

            def result(g):
                dve.wait_ge(out_ps, nth(1, g, 1))
                if later(g):
                    dve.wait_ge(stored, nth(16, g, 0))
                dve.tensor_tensor(res[:], out_bank(g), x2_of(g), ALU.add).then_inc(res_ok, 1)

            def step(p, a, f, g):
                if first(p):
                    dve.wait_ge(mean_q, 1)
                    for k in range(DK):
                        dve.tensor_tensor(wq_sb[:, k, :], wq_sb[:, k, :], ps_w0[:], ALU.subtract)\
                           .then_inc(wq_cent, 1)
                    dve.wait_ge(cs_ok, 4)
                    rotate_k(p)
                    split_lo(wq_lo, wq_sb, wq_hi, wq_h, wq_l, 1)
                    statistics1(p)
                    k_low(p)
                    split_lo(wq_lo, wq_sb, wq_hi, wq_h, wq_l, 2)
                    dve.wait_ge(stat1, 1)
                    variance1(p)
                    split_lo(wq_lo, wq_sb, wq_hi, wq_h, wq_l, 3)
                    q_table(p)
                    rotate_q(p)
                    am_centre(slice(0, HALF), MEAN_A, 1)
                    q_low(p, 0)
                    q_low(p, 1)
                    return
                top(a, 0)
                top(a, 1)
                if first(a):
                    statistics1(p)
                    am_centre(slice(HALF, AM), MEAN_B, 2)
                    dve.wait_ge(stat1, nth(3, p, 1))
                    invert(a, 0)
                    variance1(p)
                    rotate_k(p)
                    top(a, 2)
                    q_table(p)
                    invert(a, 1)
                    k_low(p)
                    top(a, 3)
                    dve.wait_ge(am_cent, 2 * DK)
                    split_am(0)
                    rotate_q(p, lambda: invert(a, 2))
                    split_am(1)
                    invert(a, 3)
                    q_low(p, 0)
                    q_low(p, 1)
                    o_low(a, 0)
                    split_am(2)
                    split_am(3)
                    return
                if g is not None:
                    z_low(g)
                o_low(f, 1)
                rotate_k(p)
                invert(a, 0)
                statistics1(p)
                if g is not None:
                    result(g)
                if first(f):
                    dve.wait_ge(ld["b"], 16)
                    for k in range(DK):
                        split_hi(b_sb, b_hi, b_h, k)
                dve.wait_ge(stat1, nth(3, p, 1))
                top(a, 2)
                variance1(p)
                invert(a, 1)
                k_low(p)
                if first(f):
                    split_lo(b_lo, b_sb, b_hi, b_h, b_l2, 2)
                residual(f)
                top(a, 3)
                invert(a, 2)
                statistics2(f)
                q_table(p)
                variance2(f)
                if first(f):
                    split_lo(b_lo, b_sb, b_hi, b_h, b_l2, 3)
                x2_low(f)
                rotate_q(p, lambda: invert(a, 3))
                o_low(a, 0)
                route(f, lambda: q_low(p, 0))
                gated(f)
                q_low(p, 1)

            def finish(p, a, f, g):
                o_low(f, 1)
                top(a, 0)
                top(a, 1)
                shift(a, 1)
                invert(a, 0)
                residual(f)
                sum_up(a, 1, 1)
                invert(a, 1)
                top(a, 2)
                z_low(g)
                top(a, 3)
                shift(a, 3)
                x2_low(f)
                invert(a, 2)
                statistics2(f)
                variance2(f)
                sum_up(a, 3, 2)
                invert(a, 3)
                result(g)
                route(f, lambda: o_low(a, 0))
                gated(f)
                o_low(a, 1)
                z_low(f)
                residual(a)
                statistics2(a)
                variance2(a)
                x2_low(a)
                result(f)
                route(a, lambda: None)
                gated(a)
                z_low(a)
                result(a)

            pipeline(dve, step, finish)

        @block.tensor
        def _(pe):
            def product(dst, hi, lo, w_hi, w_lo, cols, chunks=range(DK)):
                for k in chunks:
                    pe.matmul(dst, hi(k), w_hi[:, k, cols], start=(k == 0), stop=False)
                    pe.matmul(dst, hi(k), w_lo[:, k, cols], start=False, stop=False)
                    mm = pe.matmul(dst, lo(k), w_hi[:, k, cols], start=False, stop=(k == DK - 1))
                return mm

            def chunk(t):
                return lambda k: t[:, k, :]

            def turn(dst, src, n):
                for k in range(n):
                    mm = pe.transpose(dst[:, P * k:P * (k + 1)], src[:, P * k:P * (k + 1)], ident[:])
                return mm

            def keep_warm(bank, n):
                for _ in range(n):
                    pe.matmul(bank, warm[:, 0:P], warm[:], start=True, stop=True)

            pe.wait_ge(warm_ok, 1)
            keep_warm(ps_t0[:], WARM)

            def scores(a, u):
                b, rp = u // 2, u % 2
                if rp == 0:
                    pe.wait_ge(qT_hi_ok, nth(1, a, 1))
                    pe.wait_ge(qT_lo_ok, nth(2, a, b + 1))
                    pe.wait_ge(k_bd_ok, nth(2, a, 2))
                if later(a) or u >= 2:
                    pe.wait_ge(exp_ok, nth(U, a, u - 1))
                dst = ps_s[:, u % 2, :]
                q_hi, q_lo = (q[:, b, 2 * rp:2 * rp + 2, :].rearrange("p r q -> p (r q)") for q in (qT_hi, qT_lo))
                k_hi, k_lo = (k[:, b].rearrange("p h k -> p (h k)") for k in (k_bd_hi, k_bd_lo))
                pe.matmul(dst, q_hi, k_hi, start=True, stop=False)
                pe.matmul(dst, q_hi, k_lo, start=False, stop=False)
                pe.matmul(dst, q_lo, k_hi, start=False, stop=True).then_inc(s_ps, 1)

            def turn_unit(a, u):
                pe.wait_ge(prob_ok, nth(U, a, u + 1))
                if later(a) or u >= 1:
                    pe.wait_ge(pT_ok, nth(U, a, u))
                else:
                    pe.wait_ge(am_cent, 2 * DK)
                turn(ps_d, prob[:, u % 2, :], PAIRS).then_inc(pT_ps, 1)

            def values(a, b):
                pe.wait_ge(pT_ok, nth(U, a, 2 * b + 2))
                pe.wait_ge(v_bd_ok, nth(4, a, 4))
                if b == 1 or later(a):
                    pe.wait_ge(oT_lo_ok, nth(2, a, b))
                else:
                    pe.wait_ge(route_w, 2)
                for c in range(PAIRS):
                    mm = pe.matmul(ps_o[32 * c:32 * c + 32, b, :], v_bd[:, b, c, :], pT[:, b, c, :],
                                   start=True, stop=True)
                mm.then_inc(o_ps, 1)

            def project_kv(p):
                pe.wait_ge(c_hi_ok, nth(1, p, 1))
                pe.wait_ge(c_lo_ok, nth(1, p, 1))
                product(ps_w1[:, 0:2 * KV], chunk(cT_hi), chunk(cT_lo), wkv_hi, wkv_lo, slice(0, 2 * KV))\
                    .then_inc(kv_ps, 1)

            def turn_k(p):
                pe.wait_ge(k_rot, nth(3, p, 3))
                pe.transpose(ps_t1[:, 0:P], k_r[:], ident[:]).then_inc(kT_ps, 1)

            def project_q(chunks):
                return product(ps_w0[:], chunk(xT_hi), chunk(xT_lo), wq_hi, wq_lo, slice(0, D), chunks)

            def turn_q(p):
                pe.wait_ge(q_r_ok, nth(1, p, 1))
                turn(ps_t0, q_r, REP).then_inc(qT_ps, 1)

            def mean_down(dst, cols):
                for k in range(DK):
                    mm = pe.matmul(dst, mean_w[:], am_sb[:, k, cols], start=(k == 0), stop=(k == DK - 1))
                mm.then_inc(mean_am, 1)

            def project_out(f):
                if first(f):
                    pe.wait_ge(wo_h, REP)
                    pe.wait_ge(wo_l, REP)
                pe.wait_ge(oT_hi_ok, nth(2, f, 2))
                pe.wait_ge(oT_lo_ok, nth(2, f, 2))
                product(y_bank(f), *(lambda k, o=o: o[:, k].rearrange("p b q -> p (b q)") for o in (oT_hi, oT_lo)),
                        wo_hi, wo_lo, slice(0, D)).then_inc(y_ps, 1)

            def turn_x2(f):
                pe.wait_ge(x2_ok, nth(1, f, 1))
                turn(ps_t0, x2_of(f), DK).then_inc(x2T_ps, 1)

            def project_down(f, half):
                if half == 0:
                    if first(f):
                        pe.wait_ge(am_h, DK)
                        pe.wait_ge(am_l, DK)
                    pe.wait_ge(x2T_hi_ok, nth(1, f, 1))
                    pe.wait_ge(x2T_lo_ok, nth(1, f, 1))
                product(z_bank(f, half)[:, 0:HALF], chunk(x2T_hi), chunk(x2T_lo), am_hi, am_lo,
                        slice(HALF * half, HALF * (half + 1))).then_inc(z_ps, 1)

            def turn_zg(g):
                pe.wait_ge(zg_ok, nth(2, g, 2))
                turn(ps_t1, zg, DK).then_inc(zT_ps, 1)

            def project_up(g, chunks=range(DK)):
                if first(g):
                    pe.wait_ge(b_l, 2)
                    pe.wait_ge(b_l2, 2)
                pe.wait_ge(zT_hi_ok, nth(2, g, 2))
                for k in chunks:
                    if k % 2 == 0:
                        pe.wait_ge(zT_lo_ok, nth(2, g, k // 2 + 1))
                    mm = product(out_bank(g), chunk(zT_hi), chunk(zT_lo), b_hi, b_lo, slice(0, D), [k])
                if k == DK - 1:
                    mm.then_inc(out_ps, 1)

            def start_up():
                pe.wait_ge(const_ok, 1)
                for k in range(DK):
                    pe.wait_ge(ld_wq[k], 16)
                    mm = pe.matmul(ps_w0[:], mean_w[:], wq_sb[:, k, :], start=(k == 0), stop=(k == DK - 1))
                mm.then_inc(mean_q, 1)
                pe.wait_ge(ld["router"], 16)
                for k in range(DK):
                    mm = pe.matmul(ROUTE[:, E * k:E * (k + 1)], router_sb[:, P * k:P * (k + 1)],
                                   router_sb[:, D:D + E], start=True, stop=True)
                mm.then_inc(route_w, 1)
                pe.wait_ge(wkv_l, 1)
                project_kv(0)
                pe.wait_ge(const_ok, 12)
                turn_k(0)
                pe.wait_ge(x_hi_ok, 1)
                pe.wait_ge(x_lo_ok, 1)
                pe.wait_ge(wq_l0, 1)
                project_q([0])
                for k in range(1, DK):
                    pe.wait_ge(wq_l, k)
                    mm = project_q([k])
                mm.then_inc(q_ps, 1)
                pe.wait_ge(ld["am"], 16)
                pe.wait_ge(route_w, 2)
                pe.wait_ge(v_st_ok, 1)
                mean_down(MEAN_A, slice(0, HALF))
                turn_q(0)

            def step(p, a, f, g):
                if first(p):
                    start_up()
                    return
                scores(a, 0)
                scores(a, 1)
                if g is not None:
                    pe.wait_ge(kT_lo_ok, nth(1, p, 0))
                    turn_zg(g)
                if first(a):
                    mean_down(MEAN_B, slice(HALF, AM))
                    pe.wait_ge(am_cent, DK)
                    project_kv(p)
                    pe.wait_ge(x_hi_ok, 2)
                    pe.wait_ge(x_lo_ok, 2)
                    pe.wait_ge(q_rot, 2)
                    scores(a, 2)
                    project_q(range(DK // 2))
                elif g is None:
                    pe.wait_ge(v_st_ok, nth(1, p, 0))
                    project_kv(p)
                    pe.wait_ge(x_hi_ok, nth(1, p, 1))
                    pe.wait_ge(x_lo_ok, nth(1, p, 1))
                    pe.wait_ge(q_rot, nth(2, p, 0))
                    project_q(range(DK // 2))
                else:
                    pe.wait_ge(zg_ok, nth(2, g, 1))
                    project_kv(p)
                    project_up(g)
                if later(a):
                    scores(a, 2)
                if g is not None:
                    pe.wait_ge(zT_lo_ok, nth(2, g, 2))
                else:
                    pe.wait_ge(kT_lo_ok, nth(1, p, 0))
                turn_k(p)
                if first(a):
                    scores(a, 3)
                turn_unit(a, 0)
                if first(a):
                    project_q(range(DK // 2, DK)).then_inc(q_ps, 1)
                else:
                    pe.wait_ge(v_st_ok, nth(1, p, 1))
                    project_out(f)
                    scores(a, 3)
                turn_unit(a, 1)
                if first(a):
                    turn_q(p)
                else:
                    if g is not None:
                        pe.wait_ge(x_hi_ok, nth(1, p, 1))
                        pe.wait_ge(x_lo_ok, nth(1, p, 1))
                        pe.wait_ge(res_ok, nth(1, g, 1))
                        project_q(range(DK // 2))
                    pe.wait_ge(qT_lo_ok, nth(2, p, 0))
                    turn_x2(f)
                    project_q(range(DK // 2, DK)).then_inc(q_ps, 1)
                turn_unit(a, 2)
                values(a, 0)
                if f is not None:
                    project_down(f, 0)
                turn_unit(a, 3)
                if f is not None:
                    pe.wait_ge(x2T_lo_ok, nth(1, f, 1))
                    turn_q(p)
                    pe.wait_ge(q_rot, nth(2, p, 2))
                    project_down(f, 1)
                values(a, 1)

            def finish(p, a, f, g):
                scores(a, 0)
                scores(a, 1)
                pe.wait_ge(kT_lo_ok, T)
                turn_zg(g)
                pe.wait_ge(zg_ok, nth(2, g, 1))
                project_out(f)
                scores(a, 2)
                scores(a, 3)
                turn_unit(a, 0)
                pe.wait_ge(qT_lo_ok, 2 * T)
                turn_x2(f)
                turn_unit(a, 1)
                project_up(g)
                project_down(f, 0)
                turn_unit(a, 2)
                values(a, 0)
                turn_unit(a, 3)
                pe.wait_ge(res_ok, nth(1, g, 1))
                project_down(f, 1)
                values(a, 1)
                turn_zg(f)
                pe.wait_ge(exp_ok, U * T)
                project_out(a)
                project_up(f, range(DK // 2))
                turn_x2(a)
                project_up(f, range(DK // 2, DK))
                project_down(a, 0)
                project_down(a, 1)
                keep_warm(ps_s[:, 1, :], 8)
                turn_zg(a)
                keep_warm(ps_s[:, 1, :], 5)
                project_up(a)

            pipeline(pe, step, finish)


def kernel(x, ctx_4096, itok_BxS2_0_2047, L0_xattn_Wq, L0_xattn_Wk, L0_xattn_Wv, L0_xattn_Wo,
           L0_ffn_A_w, L0_ffn_B_w, L0_ffn_Wq_w, L0_ffn_keys):
    import concourse.bacc as bacc
    from concourse.bass_utils import run_bass_kernel_spmd

    def rows(w):
        return w.reshape(DK, P, -1).transpose(1, 0, 2)

    def turned(a):
        return a.reshape(T, P, DK, P).transpose(0, 3, 2, 1)

    x, c = np.asarray(x), np.asarray(ctx_4096)
    wo = np.asarray(L0_xattn_Wo).reshape(KVH, REP, HD, D).transpose(0, 2, 1, 3).reshape(KV, REP, D)
    arrays = {
        "x": x.reshape(T, P, D),
        "xT": turned(x.reshape(TOKENS, D)),
        "cT": turned(c.reshape(TOKENS, D)),
        "pos": np.asarray(itok_BxS2_0_2047).reshape(T, P).T,
        "wq": rows(np.asarray(L0_xattn_Wq)),
        "wkv": rows(np.concatenate([np.asarray(L0_xattn_Wk), np.asarray(L0_xattn_Wv)], axis=1)),
        "wo": wo,
        "aT": rows(np.asarray(L0_ffn_A_w).T),
        "router": np.concatenate([np.asarray(L0_ffn_Wq_w), np.asarray(L0_ffn_keys).T], axis=1),
        "bT": rows(np.asarray(L0_ffn_B_w).T),
    }
    arrays = {n: np.ascontiguousarray(a) for n, a in arrays.items()}
    nc = bacc.Bacc("TRN2", target_bir_lowering=False, num_devices=1)
    ins = [nc.dram_tensor(n, a.shape, mybir.dt.from_np(a.dtype), kind="ExternalInput").ap()
           for n, a in arrays.items()]
    out = nc.dram_tensor("out", (T, P, D), F32, kind="ExternalOutput").ap()
    build(nc, *ins, out)
    r = run_bass_kernel_spmd(nc, [arrays], core_ids=[0])
    return r.results[0]["out"].reshape(16, BATCH, D)
```
